# Optimizing a Trainium2 kernel written in Bass

```python
import numpy as np
import jax
import jax.numpy as jnp

def _softmax(x, axis=-1):
    return jax.nn.softmax(x, axis=axis)

def _gelu(x):
    return jax.nn.gelu(x, approximate=True)

def _silu(x):
    return jax.nn.silu(x)

def _sigmoid(x):
    return jax.nn.sigmoid(x)

def _layernorm(x, axis=-1, eps=1e-05):
    m = jnp.mean(x, axis=axis, keepdims=True)
    v = jnp.var(x, axis=axis, keepdims=True)
    return (x - m) / jnp.sqrt(v + eps)

def _scatter_add(tgt, idx, src, axis=0):
    return tgt.at[idx].add(src)

def _segment_sum(src, seg, n):
    return jax.ops.segment_sum(src, seg, n)
kernel_name = 'mk_prb_d1_jaxref_r8_32df17'

def setup_inputs(seed: int=0):
    np.random.seed(seed)
    _w = jnp.asarray

    def _L0_attn_setup():
        import jax, jax.numpy as jnp
        import numpy as np
        EMBED_DIM = 128
        NUM_HEADS = 8
        NUM_POINTS = 4
        B, N = (4, 1024)
        key = jax.random.key(seed)
        ks = jax.random.split(key, 8)
        C, H, P = (EMBED_DIM, NUM_HEADS, NUM_POINTS)
        sc = 1.0 / np.sqrt(C)
        x = jax.random.normal(ks[0], (B, N, C), dtype=jnp.float32)
        W_off = jax.random.normal(ks[1], (C, H * P * 2), dtype=jnp.float32) * sc
        b_off = jax.random.normal(ks[2], (H * P * 2,), dtype=jnp.float32) * 0.1
        W_attn = jax.random.normal(ks[3], (C, H * P), dtype=jnp.float32) * sc
        b_attn = jax.random.normal(ks[4], (H * P,), dtype=jnp.float32) * 0.1
        W_out = jax.random.normal(ks[5], (C, C), dtype=jnp.float32) * sc
        b_out = jax.random.normal(ks[6], (C,), dtype=jnp.float32) * 0.1
        return {'x': x, 'W_off': W_off, 'b_off': b_off, 'W_attn': W_attn, 'b_attn': b_attn, 'W_out': W_out, 'b_out': b_out}
    _L0_attn_in = _L0_attn_setup()

    def _L0_ffn_setup():
        import jax, jax.numpy as jnp
        import numpy as np
        B, S, DIM = (2, 256, 128)
        HID = 256
        E, NSH, TOPK = (8, 2, 2)

        def _ffn(x, w1, w2, w3):
            return jax.nn.silu(x @ w1.T) * (x @ w3.T) @ w2.T
        key = jax.random.key(seed)
        ks = jax.random.split(key, 8)
        sc = 0.02
        return {'x': jax.random.normal(ks[0], (B, S, DIM), jnp.float32), 'router_w': jax.random.normal(ks[1], (E, DIM), jnp.float32) * sc, 'expert_bias': jnp.zeros((E,), jnp.float32), 'w1': jax.random.normal(ks[2], (E, HID, DIM), jnp.float32) * sc, 'w3': jax.random.normal(ks[3], (E, HID, DIM), jnp.float32) * sc, 'w2': jax.random.normal(ks[4], (E, DIM, HID), jnp.float32) * sc, 'sw1': jax.random.normal(ks[5], (NSH, HID, DIM), jnp.float32) * sc, 'sw3': jax.random.normal(ks[6], (NSH, HID, DIM), jnp.float32) * sc, 'sw2': jax.random.normal(ks[7], (NSH, DIM, HID), jnp.float32) * sc}
    _L0_ffn_in = _L0_ffn_setup()
    _d = {'L0_attn_x': _L0_attn_in['x'], 'L0_attn_W_off': _L0_attn_in['W_off'], 'L0_attn_b_off': _L0_attn_in['b_off'], 'L0_attn_W_attn': _L0_attn_in['W_attn'], 'L0_attn_b_attn': _L0_attn_in['b_attn'], 'L0_attn_W_out': _L0_attn_in['W_out'], 'L0_attn_b_out': _L0_attn_in['b_out'], 'L0_ffn_router_w': _L0_ffn_in['router_w'], 'L0_ffn_expert_bias': _L0_ffn_in['expert_bias'], 'L0_ffn_w1': _L0_ffn_in['w1'], 'L0_ffn_w3': _L0_ffn_in['w3'], 'L0_ffn_w2': _L0_ffn_in['w2'], 'L0_ffn_sw1': _L0_ffn_in['sw1'], 'L0_ffn_sw3': _L0_ffn_in['sw3'], 'L0_ffn_sw2': _L0_ffn_in['sw2']}
    _x0 = _d['L0_attn_x']
    _d['L0_attn_x'] = jax.random.normal(jax.random.fold_in(jax.random.key(seed), 1), (8, 1024, 128), dtype=_x0.dtype)
    del _x0
    return _d

def reference(L0_attn_x, L0_attn_W_off, L0_attn_b_off, L0_attn_W_attn, L0_attn_b_attn, L0_attn_W_out, L0_attn_b_out, L0_ffn_router_w, L0_ffn_expert_bias, L0_ffn_w1, L0_ffn_w3, L0_ffn_w2, L0_ffn_sw1, L0_ffn_sw3, L0_ffn_sw2):

    def _L0_attn_ref(x, W_off, b_off, W_attn, b_attn, W_out, b_out):
        import jax, jax.numpy as jnp
        import numpy as np
        EMBED_DIM = 128
        NUM_HEADS = 8
        NUM_POINTS = 4
        B, N = (4, 1024)
        Bx, Nx, C = x.shape
        H, P = (NUM_HEADS, NUM_POINTS)
        off = (x @ W_off + b_off).reshape(Bx, Nx, H, P, 2)
        w = jax.nn.softmax((x @ W_attn + b_attn).reshape(Bx, Nx, H, P), axis=-1)
        idx = off[..., 0].astype(jnp.int32)
        idx = jnp.where(idx < 0, idx + C, idx)
        idx = jnp.clip(idx, 0, C - 1)
        x0 = x[:, 0, :]
        g = jnp.take_along_axis(x0, idx.reshape(Bx, -1), axis=1).reshape(Bx, Nx, H, P)
        s = jnp.sum(g * w, axis=(2, 3))
        out = jnp.broadcast_to(s[..., None], (Bx, Nx, C))
        return out @ W_out + b_out

    def _L0_ffn_ref(x, router_w, expert_bias, w1, w3, w2, sw1, sw3, sw2):
        import jax, jax.numpy as jnp
        import numpy as np
        B, S, DIM = (2, 256, 128)
        HID = 256
        E, NSH, TOPK = (8, 2, 2)

        def _ffn(x, w1, w2, w3):
            return jax.nn.silu(x @ w1.T) * (x @ w3.T) @ w2.T
        bs, sl, d = x.shape
        xf = x.reshape(-1, d)
        shared = jnp.zeros_like(xf)
        for i in range(sw1.shape[0]):
            shared = shared + _ffn(xf, sw1[i], sw2[i], sw3[i])
        logits = xf @ router_w.T + expert_bias
        rw, sel = jax.lax.top_k(logits, TOPK)
        rw = jax.nn.softmax(rw.astype(jnp.float32), axis=-1).astype(x.dtype)
        onehot = jax.nn.one_hot(sel, E, dtype=x.dtype)
        combine = jnp.einsum('tk,tke->te', rw, onehot)

        def body(acc, ew):
            e1, e3, e2, cw = ew
            acc = acc + cw[:, None] * _ffn(xf, e1, e2, e3)
            return (acc, None)
        out, _ = jax.lax.scan(body, jnp.zeros_like(xf), (w1, w3, w2, combine.T))
        out = out + shared
        return out.reshape(bs, sl, -1)
    x = L0_attn_x
    xn = _layernorm(x, axis=-1)
    x = x + _L0_attn_ref(xn, L0_attn_W_off, L0_attn_b_off, L0_attn_W_attn, L0_attn_b_attn, L0_attn_W_out, L0_attn_b_out) + _L0_ffn_ref(xn, L0_ffn_router_w, L0_ffn_expert_bias, L0_ffn_w1, L0_ffn_w3, L0_ffn_w2, L0_ffn_sw1, L0_ffn_sw3, L0_ffn_sw2)
    return x

_drawn_inputs = setup_inputs


def setup_inputs(seed=0):
    import zlib

    import numpy as np

    out = dict(_drawn_inputs(seed))
    spreads = {'L0_ffn_expert_bias': (0.0, 0.8)}
    factors = {'L0_attn_b_attn': 5.415,
     'L0_attn_b_out': 4.513,
     'L0_ffn_router_w': 8.0,
     'L0_ffn_w1': 8.0,
     'L0_ffn_w3': 8.0,
     'L0_ffn_w2': 8.0,
     'L0_ffn_sw1': 8.0,
     'L0_ffn_sw3': 8.0,
     'L0_ffn_sw2': 8.0}
    for name, (base, spread) in spreads.items():
        noise = np.random.default_rng([zlib.crc32(name.encode()), seed]).standard_normal(out[name].shape)
        drawn = base * np.exp(spread * noise) if base else spread * noise
        out[name] = jnp.asarray(drawn.astype(out[name].dtype))
    for name, factor in factors.items():
        out[name] = (out[name] * factor).astype(out[name].dtype)
    return out
```

```python
from contextlib import ExitStack

import numpy as np

import concourse.bass as bass
from concourse import mybir

ALU = mybir.AluOpType
ACT = mybir.ActivationFunctionType
AX = mybir.AxisListType
F32 = mybir.dt.float32
F16 = mybir.dt.float16
I32 = mybir.dt.int32
I16 = mybir.dt.int16
U32 = mybir.dt.uint32

P = 128
BATCH, SEQ = 8, 1024
TOK = BATCH * SEQ
NT = TOK // P
BLK = 512
TPB = BLK // P
NB = TOK // BLK
HEADS, POINTS = 8, 4
HP = HEADS * POINTS
E, NSH, HID = 8, 2, 256
NE = E + NSH
NPAIR = E * (E - 1) // 2
PROJ = 2 * HP + E
NQ = 4
RING = 4
ROUTED = -(-((TOK + NPAIR * (P - 1)) // P) // RING) * RING
SLOTS = ROUTED * P
ROWW = 132
CWA, CWB, TOKW = 128, 129, 130
XS = 4096.0
WS = 64.0
EPS = 1e-5
LO16, HI16 = 16, 8
GRP = 8
NG = HP // GRP
W1, W3, W2 = 0, HID, 2 * HID
WCOL = 3 * HID


def constants():
    p = np.arange(P)
    b_of, h_of = p // GRP, p % GRP
    ah = np.arange(HI16 * GRP)
    a_of, g_of = ah // GRP, ah % GRP
    ea, eb = np.array([(a, b) for a in range(E) for b in range(a + 1, E)]).T
    token = (np.arange(NT)[None, :] // TPB) * BLK + p[:, None] * TPB + np.arange(NT)[None, :] % TPB
    pad = np.zeros((P, ROWW), np.int32)
    pad[:, TOKW] = TOK + p
    f16, f32 = np.float16, np.float32
    wide = lambda v: np.broadcast_to(v[None, :], (P, len(v)))
    return {
        "ident": np.eye(P, dtype=f16),
        "before": (p[:, None] < p[None, :]).astype(f16),
        "ones": np.ones((P, P), f16),
        "low_sel": (p[:, None] % LO16 == b_of[None, :]).astype(f16),
        "high_mask": (p[:, None] // LO16 == a_of[None, :]).astype(f16),
        "same_gather": (h_of[:, None] == g_of[None, :]).astype(f16),
        "pair_ids": wide(np.repeat(np.arange(NPAIR), NT)).astype(f16),
        "pair_step_a": wide(np.diff(ea, prepend=0)).astype(f32),
        "pair_step_b": wide(np.diff(eb, prepend=0)).astype(f32),
        "from_last": wide(E - np.arange(E)).astype(f32),
        "part": p[:, None].astype(f32),
        "token": token.astype(np.int32),
        "pad_row": pad,
        "ones32": np.ones((P, P), f32),
    }


def past(t, k):
    return not isinstance(t, int) or t >= k


def pipeline(eng, total, unroll, peel, parts, begin=lambda g: None):
    last = max(lag for lag, _ in parts)
    for s in range(unroll * peel):
        if s % unroll == 0:
            begin(s // unroll)
        for lag, part in parts:
            if s >= lag:
                part((s - lag) // unroll, (s - lag) % unroll)
    if peel < total // unroll:
        with eng.Fori(peel, total // unroll) as g:
            begin(g)
            for r in range(unroll):
                for lag, part in parts:
                    part(g + (r - lag) // unroll, (r - lag) % unroll)
    for s in range(total, total + last):
        if s % unroll == 0:
            begin(s // unroll)
        for lag, part in parts:
            if s - lag < total:
                part((s - lag) // unroll, (s - lag) % unroll)


def layer_kernel(nc, x, wall, wproj, bproj, w_out, b_out, const, out, sorted_rows, y_rows):
    with ExitStack() as ctx:
        def sb(name, shape, dt):
            return ctx.enter_context(nc.sbuf_tensor(name, shape, dt))

        def sem(name):
            return ctx.enter_context(nc.semaphore(name))

        pAB = ctx.enter_context(nc.psum_tensor("pAB", [P, 4, 512], F32))
        pA, pB = pAB[:, 0:2, :], pAB[:, 2:4, :]
        pY = ctx.enter_context(nc.psum_tensor("pY", [P, 2, 512], F32))
        pV = ctx.enter_context(nc.psum_tensor("pV", [P, 2, 512], F32))

        base = sb("base", [P, NT, P], F32)
        rows = sb("rows", [P, NT, ROWW], I32)
        xT = sb("xT", [P, NB, 2, BLK], F16)
        wsp = sb("wsp", [P, 2, NE, WCOL], F16)
        whi, wlo = wsp[:, 0], wsp[:, 1]
        wraw = sb("wraw", [P, 2, WCOL], F32)
        proj = sb("proj", [P, NT, PROJ], F32)
        wp_raw = sb("wp_raw", [P, PROJ], F32)
        wp = sb("wp", [P, 2, PROJ], F16)
        bp = sb("bp", [P, PROJ], F32)
        wo = sb("wo", [P, P], F32)
        csum = sb("csum", [P, P], F32)
        bo_raw = sb("bo_raw", [1, P], F32)
        bo = sb("bo", [P, 2, P], F16)
        units = sb("units", [P, 4, 512], F32)
        silu, hf = units[:, 0:2, :], units[:, 2:4, :]
        xs = units[:].rearrange("p r (j c) -> p r j c", j=TPB)
        h_hi = sb("h_hi", [P, 4, 512], F16)
        h_lo = sb("h_lo", [P, 4, 512], F16)
        c = {}
        hotT = sb("hotT", [P, 2, 8 * P], F16)
        for name, a in const.items():
            c[name] = (hotT[:].rearrange("p r c -> p (r c)")[:, 0:NPAIR * NT] if name == "pair_ids"
                       else sb("c_" + name, list(a.shape), a.dtype))
        stats = sb("stats", [P, NT, 6], F32)
        st = sb("st", [P, 8, NT], F32)
        rt = sb("rt", [P, 12, NT], F32)
        free_hi = whi[:, NSH:, :].rearrange("p e c -> p (e c)").bitcast(F32)
        free_lo = wlo[:, NSH:, :].rearrange("p e c -> p (e c)").bitcast(F32)
        r8 = free_hi[:, 0:4 * NT * E].rearrange("p (k t e) -> p k t e", k=4, t=NT)
        scratch_a = units[:].rearrange("p u c -> p (u c)")
        scratch_b = free_hi[:, 0:NT * HP]
        member_row = free_lo[:, NT * HP:].bitcast(F16)[:, 0:NPAIR * NT]
        member = member_row.rearrange("p (q t) -> p q t", q=NPAIR)
        pair16 = sb("pair16", [P, NT], F16)
        seg = sb("seg", [P, 8, NPAIR], F32)
        seg16 = sb("seg16", [P, NPAIR], F16)
        segi = sb("segi", [P, 2, NPAIR], I32)
        slot = sb("slot", [P, NT], I32)
        tab16 = sb("tab16", [P, 2], F16)
        tab_scr = sb("tab_scr", [P, 2, NPAIR], F32)
        tab_f = sb("tab_f", [P, 2], F32)
        experts = sb("experts", [1, P, 2], I32)
        weight = sb("weight", [P, NT * HP], F32)
        wmax = free_hi[:, NT * HP:].rearrange("p (k g) -> p k g", k=2)
        fl16 = [a[:].rearrange("p u c -> p (u c)") for a in (h_hi, h_lo)]
        idx = free_lo[:, NT * HP:].bitcast(I16)
        ilo = sb("ilo", [P, NT * HP], I16)
        ihi = sb("ihi", [P, NT * HP], I16)
        table = sb("table", [P, BATCH, 2, HI16 * GRP], F16)
        proj_row = proj[:].rearrange("p t c -> p (t c)")
        hot = proj_row[:, 0:2048].bitcast(F16).rearrange("p (g b h) -> p g b h", b=LO16, h=GRP)
        aw = proj_row[:, 2048:4096].rearrange("p (g a h) -> p g a h", a=HI16, h=GRP)
        attn = sb("attn", [P, 8], F32)
        xr = (wraw[:].rearrange("p r c -> p (r c)")[:, 0:RING * ROWW].bitcast(I32)
              .rearrange("p (r w) -> p r w", r=RING))
        meta = sb("meta", [P, RING, 4], I32)
        xrT = xT[:, 0].rearrange("p s (r c) -> p (s r) c", c=2 * P)
        yt = sb("yt", [P, RING, P], F32)
        vscr = yt[:].rearrange("p (t r) c -> p t (r c)", t=2)
        tsel = yt[:].rearrange("p r c -> p (r c)").bitcast(F16).rearrange("p (g c) -> p g c", g=BATCH * 2)
        yidx = sb("yidx", [P, RING], I32)

        y_all = rows[:, :, 0:P].bitcast(F32)
        rows16 = rows[:].bitcast(F16)
        rows32 = rows[:].bitcast(F32)
        xr16 = xr.bitcast(F16)
        meta32 = meta[:].bitcast(F32)
        pY16, pV16 = pY[:].bitcast(F16), pV[:].bitcast(F16)
        pT16 = pV16[:, 0, 0:2 * P]
        pS = pV[:, 1, 0:2 * P]

        x_in = [sem(f"x_in{q}") for q in range(NQ)]
        w_in = [sem("w_in0"), sem("w_in1")]
        const_in = sem("const_in")
        pad_out = sem("pad_out")
        w_split_hi = sem("w_split_hi")
        w_split = sem("w_split")
        wp_hi = sem("wp_hi")
        small_split = sem("small_split")
        pool_go = sem("pool_go")
        bo_zero = sem("bo_zero")
        stats_done = sem("stats_done")
        dv = sem("dv")
        var_ready = sem("var_ready")
        root_ready = sem("root_ready")
        xs_ready = sem("xs_ready")
        rows_hi = sem("rows_hi")
        rows_lo = sem("rows_lo")
        turned = sem("turned")
        xt_ready = sem("xt_ready")
        proj_done = sem("proj_done")
        proj_read = sem("proj_read")
        meta_init = sem("meta_init")
        scratch_free = sem("scratch_free")
        gap_ready = sem("gap_ready")
        gap_exp = sem("gap_exp")
        cw_ready = sem("cw_ready")
        seg_ready = sem("seg_ready")
        seg_done = sem("seg_done")
        slot_ready = sem("slot_ready")
        tab_ready = sem("tab_ready")
        tab_done = sem("tab_done")
        experts_ready = sem("experts_ready")
        logit_ready = sem("logit_ready")
        logit_exp = sem("logit_exp")
        tsel_ready = sem("tsel_ready")
        table_done = sem("table_done")
        table_ready = sem("table_ready")
        csum_done = sem("csum_done")
        sorted_in = sem("sorted_in")
        l1 = sem("l1")
        silu_done = sem("silu_done")
        hf_done = sem("hf_done")
        hi_done = sem("hi_done")
        lo_done = sem("lo_done")
        l2 = sem("l2")
        y_read = sem("y_read")
        hot_ready = sem("hot_ready")
        aw_ready = sem("aw_ready")
        hot_turned = sem("hot_turned")
        hotT_ready = sem("hotT_ready")
        v_done = sem("v_done")
        v_read = sem("v_read")
        attn_added = sem("attn_added")
        d_in = [sem(f"d_in{r}") for r in range(RING)]
        d_turn = sem("d_turn")
        d_meta = sem("d_meta")
        d_xt = sem("d_xt")
        d_l1 = sem("d_l1")
        d_silu = sem("d_silu")
        d_hf = sem("d_hf")
        d_hi = sem("d_hi")
        d_lo = sem("d_lo")
        d_hturn = sem("d_hturn")
        d_hT_hi = sem("d_hT_hi")
        d_hT_lo = sem("d_hT_lo")
        d_l2 = sem("d_l2")
        d_y = sem("d_y")
        d_out = [sem(f"d_out{r}") for r in range(RING)]
        y_in = [sem(f"y_in{r}") for r in range(4)]
        fin = sem("fin")
        out_done = sem("out_done")

        n_const = len(const) + 4
        x_blk = x.rearrange("b (k p j) c -> (b k) p (j c)", p=P, j=TPB)
        out_blk = out.rearrange("b (k p j) c -> (b k) p (j c)", p=P, j=TPB)
        base_blk = base[:].rearrange("p (i j) c -> p i (j c)", j=TPB)
        sorted_tiles = sorted_rows.rearrange("(t p) w -> t p w", p=P)
        y_blk = y_rows.rearrange("(i p j) c -> i p j c", p=P, j=TPB)

        block = ctx.enter_context(nc.Block())

        @block.sync
        def _(sp):
            for q in range(NQ):
                sp.dma_start(base_blk[:, NB // NQ * q:NB // NQ * (q + 1), :],
                             x_blk[NB // NQ * q:NB // NQ * (q + 1)].rearrange("i p w -> p i w")).then_inc(x_in[q], 16)
            sp.wait_ge(const_in, 16 * n_const)
            sp.dma_start(sorted_rows.rearrange("(t p) w -> p t w", p=P),
                         c["pad_row"][:].unsqueeze(1).broadcast_to([P, ROUTED, ROWW])).then_inc(pad_out, 16)

            with sp.Fori(1, NE // 2) as g:
                for r in range(2):
                    sp.wait_ge(w_split, 2 * g + r - 1)
                    sp.dma_start(wraw[:, r, :], wall[bass.ds(2 * g + r, 1)].rearrange("o p w -> p (o w)")
                                 ).then_inc(w_in[r], 16)

            sp.wait_ge(sorted_in, 16 * NT)
            for r in range(RING):
                sp.dma_start(xr[:, r, :], sorted_tiles[r]).then_inc(d_in[r], 16)
            with sp.Fori(1, ROUTED // RING) as g:
                for r in range(RING):
                    sp.wait_ge(d_turn, RING * g + (r + 1 - RING))
                    sp.wait_ge(d_meta, RING * g + (r + 1 - RING))
                    sp.dma_start(xr[:, r, :], sorted_tiles[bass.ds(RING * g + r, 1)].rearrange("o p w -> p (o w)")
                                 ).then_inc(d_in[r], 16)

            for r in range(RING):
                sp.wait_ge(d_out[r], 16 * (ROUTED // RING))
            for r in range(4):
                sp.dma_start(y_all[:, TPB * r:TPB * r + TPB, :], y_blk[r]).then_inc(y_in[r], 16)
            with sp.Fori(1, NB // 4) as q:
                for r in range(4):
                    sp.wait_ge(y_in[r], 16 * q)
                    sp.dma_start(y_all[:, bass.ds(16 * q + 4 * r, TPB), :],
                                 y_blk[bass.ds(4 * q + r, 1)].rearrange("o p j c -> p (o j) c")).then_inc(y_in[r], 16)

        @block.tensor
        def _(pe):
            pe.wait_ge(const_in, 16 * n_const)
            pe.matmul(pY[:, 1, 0:P], c["ones32"][:], wo[:], start=True, stop=True).then_inc(csum_done, 1)

            def turn(g, r):
                i = 4 * g + r
                pe.wait_ge(rows_lo, i + 1)
                if past(i, 2):
                    pe.wait_ge(xt_ready, i - 1)
                for bank, off in ((pA, 0), (pB, P)):
                    for j in range(TPB):
                        mm = pe.matmul(bank[:, r % 2, j * P:(j + 1) * P],
                                       rows16[:, bass.ds(TPB * i + j, 1), off:off + P].rearrange("p o c -> p (o c)"),
                                       c["ident"][:], start=True, stop=True)
                mm.then_inc(turned, 1)

            def project(g, r):
                i = 4 * g + r
                pe.wait_ge(xt_ready, i + 1)
                if past(i, 2):
                    pe.wait_ge(proj_read, i - 1)
                for j in range(TPB):
                    for m, (s, w) in enumerate(((0, 0), (0, 1), (1, 0), (1, 1))):
                        mm = pe.matmul(pV[:, r % 2, j * PROJ:(j + 1) * PROJ],
                                       xT[:, bass.ds(i, 1), s, j * P:(j + 1) * P].rearrange("p o c -> p (o c)"),
                                       wp[:, w, :], start=(m == 0), stop=(m == 3))
                mm.then_inc(proj_done, 1)

            pe.wait_ge(small_split, 1)
            pipeline(pe, NB, 4, 4, [(0, turn), (1, project)])

            pe.wait_ge(seg_ready, 1)
            pe.matmul(pY[:, 0, 0:NPAIR], c["before"][:], seg16[:], start=True, stop=True)
            pe.matmul(pY[:, 0, 32:32 + NPAIR], c["ones"][:], seg16[:], start=True, stop=True).then_inc(seg_done, 1)
            pe.wait_ge(tab_ready, 1)
            for k in range(2):
                mm = pe.matmul(pY[0:1, 0, (k + 1) * P:(k + 2) * P], tab16[:, k:k + 1], c["ident"][:],
                               start=True, stop=True)
            mm.then_inc(tab_done, 1)
            pe.wait_ge(tsel_ready, 1)
            for k in range(2):
                mm = pe.matmul(pV[:, k, :], c["low_sel"][:],
                               tsel[:, 8 * k:8 * k + 8, :].rearrange("p b c -> p (b c)"), start=True, stop=True)
            mm.then_inc(table_done, 1)

            def first_products(b, u):
                n, x, h = 8 * b + u, (u // 2) % 2, u % 2
                if past(n, 2):
                    pe.wait_ge(hf_done, n - 1)
                xi = lambda s: xT[:, bass.ds(2 * b + u // 4, 1), s, :].rearrange("p o c -> p (o c)")
                for bank, col in ((pA, W1), (pB, W3)):
                    w = slice(col + h * P, col + (h + 1) * P)
                    pe.matmul(bank[:, u % 2, :], whi[:, x, w], xi(0), start=True, stop=False)
                    pe.matmul(bank[:, u % 2, :], whi[:, x, w], xi(1), start=False, stop=False)
                    mm = pe.matmul(bank[:, u % 2, :], wlo[:, x, w], xi(0), start=False, stop=True)
                mm.then_inc(l1, 1)

            def second_products(b, u):
                n, i, x, h = 8 * b + u, 2 * b + u // 4, (u // 2) % 2, u % 2
                w = slice(W2 + h * P, W2 + (h + 1) * P)
                if u % 4 == 0 and past(i, 2):
                    pe.wait_ge(y_read, i - 1)
                pe.wait_ge(lo_done, n + 1)
                for j in range(TPB):
                    o, t = pY[:, u // 4, j * P:(j + 1) * P], slice(j * P, (j + 1) * P)
                    if u % 4 == 0:
                        pe.matmul(o, c["ones"][:], bo[:, 0, :], start=(j == 0), stop=False, skip_group_check=True)
                        pe.matmul(o, c["ones"][:], bo[:, 1, :], start=False, stop=False, skip_group_check=True)
                    for m, (hid, wt) in enumerate(((h_hi, whi), (h_hi, wlo), (h_lo, whi))):
                        mm = pe.matmul(o, hid[:, u % 4, t], wt[:, x, w], start=False,
                                       stop=(u % 4 == 3 and m == 2), skip_group_check=True)
                mm.then_inc(l2, 1)

            def attention(b, u):
                r = u // 2
                if u % 2 == 0:
                    if r == 0:
                        pe.wait_ge(hot_ready, b + 1)
                    if past(8 * b + u, 1):
                        pe.wait_ge(hotT_ready, 4 * b + r)
                    for k in range(8):
                        mm = pe.transpose(pV16[:, 0, k * P:(k + 1) * P],
                                          hot[:, 8 * r + k, :, :].rearrange("p b h -> p (b h)"), c["ident"][:])
                    mm.then_inc(hot_turned, 1)
                else:
                    pe.wait_ge(hotT_ready, 4 * b + r + 1)
                    if past(8 * b + u, 2):
                        pe.wait_ge(v_read, 4 * b + r)
                    for k in range(8):
                        for s in range(2):
                            mm = pe.matmul(pV[:, 1, k * 64:(k + 1) * 64], hotT[:, r % 2, k * P:(k + 1) * P],
                                           table[:, bass.ds(b, 1), s, :].rearrange("p o c -> p (o c)"),
                                           start=(s == 0), stop=(s == 1))
                    mm.then_inc(v_done, 1)

            pe.wait_ge(w_split, NE)
            pe.wait_ge(small_split, 2)
            pe.wait_ge(experts_ready, 1)
            pe.wait_ge(table_ready, 1)
            pipeline(pe, 4 * NB, 8, 1, [(0, first_products), (0, attention), (2, second_products)])

            pe.wait_ge(y_read, NB)
            pe.wait_ge(v_read, 4 * BATCH)

            pairs = []

            def load_pairs(g):
                n = 2 * RING if past(g, 1) else RING
                _, values = nc.values_load_multi_w_load_instructions(
                    experts[0:1, bass.ds(RING * g + RING - n, n), :].rearrange("p t k -> p (t k)"),
                    engines=(mybir.EngineType.PE,), min_val=NSH, max_val=NE - 1,
                    skip_runtime_bounds_check_because="the table's entries are NSH plus sums of steps between experts")
                pairs[:] = [None] * (2 * RING - n) + [values[2 * i:2 * i + 2] for i in range(n)]

            def r_turn(g, r):
                t = RING * g + r
                pe.wait_ge(d_in[r], 16 * (g + 1))
                for s in range(2):
                    mm = pe.transpose(pT16[:, s * P:(s + 1) * P], xr16[:, r, s * P:(s + 1) * P], c["ident"][:])
                mm.then_inc(d_turn, 1)

            def r_first(g, r):
                t = RING * g + r
                pe.wait_ge(d_xt, t + 1)
                for k, e in enumerate(pairs[RING - 1 if r == RING - 1 else RING + r]):
                    o = pAB[:, 2 * (r % 2) + k, :]
                    hi, lo = (wsp[:, s, bass.ds(e, 1), 0:2 * HID].rearrange("p o c -> p (o c)") for s in range(2))
                    pe.matmul(o, xrT[:, r, 0:P], hi, start=True, stop=False)
                    pe.matmul(o, xrT[:, r, P:2 * P], hi, start=False, stop=False)
                    mm = pe.matmul(o, xrT[:, r, 0:P], lo, start=False, stop=True)
                mm.then_inc(d_l1, 1)

            def r_hturn(g, r):
                t = RING * g + r
                pe.wait_ge(d_lo, t + 1)
                for s, part in enumerate((h_hi, h_lo)):
                    for k in range(4):
                        mm = pe.transpose(pY16[:, s, k * P:(k + 1) * P],
                                          part[:, r % 2, k * P:(k + 1) * P], c["ident"][:])
                mm.then_inc(d_hturn, 1)

            def r_second(g, r):
                t = RING * g + r
                pe.wait_ge(d_hT_hi, t + 1)
                pe.wait_ge(d_hT_lo, t + 1)
                for k, e in enumerate(pairs[r]):
                    for h in range(2):
                        w = slice(W2 + h * P, W2 + (h + 1) * P)
                        q = 2 * k + h
                        both = wsp[:, :, bass.ds(e, 1), w].rearrange("p s o c -> p s (o c)")
                        hi = wsp[:, 0, bass.ds(e, 1), w].rearrange("p o c -> p (o c)")
                        pe.matmul(pS.rearrange("p (s c) -> p s c", s=2),
                                  h_hi[:, 2 + r % 2, q * P:(q + 1) * P], both,
                                  start=(q == 0), stop=False, skip_group_check=True)
                        mm = pe.matmul(pS[:, 0:P], h_lo[:, 2 + r % 2, q * P:(q + 1) * P], hi,
                                       start=False, stop=(q == 3), skip_group_check=True)
                mm.then_inc(d_l2, 1)

            pipeline(pe, ROUTED, RING, 2, [(4, r_second), (3, r_hturn), (1, r_first), (0, r_turn)], begin=load_pairs)

        @block.scalar
        def _(act):
            for dst, src in [(wp_raw[:], wproj), (bp[:], bproj), (wo[:], w_out), (bo_raw[:], b_out)] + [
                    (c[k] if k == "pair_ids" else c[k][:], const[k]) for k in const]:
                act.dma_start(dst, src).then_inc(const_in, 16)
            for r in range(2):
                act.dma_start(wraw[:, r, :], wall[r]).then_inc(w_in[r], 16)
            act.wait_ge(const_in, 16 * n_const)
            nc.scalar.activation(wp[:, 0, :], wp_raw[:], ACT.Copy, scale=WS).then_inc(wp_hi, 1)
            act.wait_ge(bo_zero, 1)

            def split_high(g, r):
                act.wait_ge(w_in[r], 16 * (g + 1))
                nc.scalar.activation(whi[:, bass.ds(2 * g + r, 1), :].rearrange("p o c -> p (o c)"),
                                     wraw[:, r, :], ACT.Copy, scale=WS).then_inc(w_split_hi, 1)

            nc.scalar.activation(bo[0:1, 0, :], bo_raw[:], ACT.Copy, scale=WS).then_inc(wp_hi, 1)
            act.wait_ge(var_ready, 1)
            nc.scalar.activation(st[:, 5, :], st[:, 4, :], ACT.Sqrt).then_inc(root_ready, 1)

            def rows_high(g, r):
                i = 4 * g + r
                act.wait_ge(xs_ready, i + 1)
                nc.scalar.copy(rows16[:, bass.ds(TPB * i, TPB), 0:P], xs[:, r, :, :]).then_inc(rows_hi, 1)

            def turned_copy(g, r):
                i = 4 * g + r
                act.wait_ge(turned, i + 1)
                for s, bank in enumerate((pA, pB)):
                    a = nc.scalar.copy(xT[:, bass.ds(i, 1), s, :].rearrange("p o c -> p (o c)"), bank[:, r % 2, :])
                a.then_inc(xt_ready, 1)

            pipeline(act, NB, 4, 4, [(0, rows_high), (2, turned_copy)])
            for r in range(NSH):
                split_high(0, r)

            act.wait_ge(gap_ready, 1)
            nc.scalar.activation(rt[:, 5, :], rt[:, 4, :], ACT.Exp).then_inc(gap_exp, 1)
            act.wait_ge(logit_ready, 1)
            nc.scalar.activation(weight[:], weight[:], ACT.Exp).then_inc(logit_exp, 1)

            act.wait_ge(scratch_free, 1)
            with act.Fori(1, NE // 2) as g:
                for r in range(2):
                    split_high(g, r)

            def silu_unit(b, u):
                n = 8 * b + u
                act.wait_ge(l1, n + 1)
                if past(n, 2):
                    act.wait_ge(hf_done, n - 1)
                nc.scalar.activation(silu[:, u % 2, :], pA[:, u % 2, :], ACT.Silu,
                                     scale=1 / (XS * WS)).then_inc(silu_done, 1)

            def hi_unit(b, u):
                n = 8 * b + u
                act.wait_ge(hf_done, n + 1)
                if past(n, 4):
                    act.wait_ge(l2, n - 3)
                nc.scalar.copy(h_hi[:, u % 4, :], hf[:, u % 2, :]).then_inc(hi_done, 1)

            def hot_copy(b, u):
                if u % 2 == 0:
                    r = u // 2
                    act.wait_ge(hot_turned, 4 * b + r + 1)
                    if past(8 * b + u, 3):
                        act.wait_ge(v_done, 4 * b + r - 1)
                    nc.scalar.copy(hotT[:, r % 2, :], pV16[:, 0, :]).then_inc(hotT_ready, 1)

            pipeline(act, 4 * NB, 8, 1, [(0, silu_unit), (0, hot_copy), (1, hi_unit)])

            act.wait_ge(hf_done, 4 * NB)
            act.wait_ge(l2, 4 * NB)

            def r_xt(g, r):
                t = RING * g + r
                act.wait_ge(d_turn, t + 1)
                nc.scalar.copy(xrT[:, r, :], pT16).then_inc(d_xt, 1)

            def r_silu(g, r):
                t = RING * g + r
                act.wait_ge(d_l1, t + 1)
                nc.scalar.activation(silu[:, r % 2, :].rearrange("p (k c) -> p k c", k=2),
                                     pAB[:, 2 * (r % 2):2 * (r % 2) + 2, 0:HID], ACT.Silu,
                                     scale=1 / (XS * WS)).then_inc(d_silu, 1)

            def r_hi(g, r):
                t = RING * g + r
                act.wait_ge(d_hf, t + 1)
                nc.scalar.copy(h_hi[:, r % 2, :], hf[:, r % 2, :]).then_inc(d_hi, 1)

            def r_hT_hi(g, r):
                t = RING * g + r
                act.wait_ge(d_hturn, t + 1)
                nc.scalar.copy(h_hi[:, 2 + r % 2, :], pY16[:, 0, 0:512]).then_inc(d_hT_hi, 1)

            pipeline(act, ROUTED, RING, 2, [(2, r_silu), (1, r_xt), (2, r_hi), (3, r_hT_hi)])

            with act.Fori(0, NB) as i:
                act.wait_ge(fin, i + 1)
                act.dma_start(out_blk[bass.ds(i, 1)].rearrange("o p w -> p (o w)"),
                              base_blk[:, bass.ds(i, 1), :].rearrange("p o w -> p (o w)")).then_inc(out_done, 16)
            act.wait_ge(out_done, 16 * NB)

        @block.gpsimd
        def _(pool):
            nc.gpsimd.memset(bo[:], 0.0).then_inc(bo_zero, 1)
            nc.gpsimd.memset(rows[:, :, 2 * P // 2:ROWW], 0).then_inc(meta_init, 1)
            pool.wait_ge(const_in, 16 * n_const)
            pool.wait_ge(meta_init, 1)
            nc.gpsimd.tensor_copy(rows[:, :, TOKW:TOKW + 1], c["token"][:].unsqueeze(2)).then_inc(meta_init, 1)

            def rows_low(g, r):
                i = 4 * g + r
                pool.wait_ge(rows_hi, i + 1)
                pool.sem_inc(pool_go, 1)
                nc.gpsimd.tensor_tensor(rows16[:, bass.ds(TPB * i, TPB), P:2 * P], xs[:, r, :, :],
                                        rows16[:, bass.ds(TPB * i, TPB), 0:P], ALU.subtract).then_inc(rows_lo, 1)

            pipeline(pool, NB, 4, 1, [(0, rows_low)])

            pool.wait_ge(slot_ready, 1)
            pool.wait_ge(cw_ready, 1)
            pool.wait_ge(pad_out, 16)
            for n in range(4 * NB):
                pool.indirect_dma_start(sorted_rows, bass.IndirectOffsetOnAxis(ap=slot[:, n:n + 1].bitcast(U32), axis=0),
                                        rows[:, n, :], None, bounds_check=SLOTS - 1).then_inc(sorted_in, 16)
                pool.wait_ge(hi_done, n + 1)
                nc.gpsimd.tensor_tensor(h_lo[:, n % 4, :], hf[:, n % 2, :], h_hi[:, n % 4, :],
                                        ALU.subtract).then_inc(lo_done, 1)

            def r_lo(g, r):
                t = RING * g + r
                pool.wait_ge(d_hi, t + 1)
                pool.sem_inc(pool_go, 1)
                nc.gpsimd.tensor_tensor(h_lo[:, r % 2, :], hf[:, r % 2, :], h_hi[:, r % 2, :],
                                        ALU.subtract).then_inc(d_lo, 1)

            def r_scatter(g, r):
                pool.wait_ge(d_y, RING * g + r + 1)
                pool.sem_inc(pool_go, 1)
                pool.indirect_dma_start(y_rows, bass.IndirectOffsetOnAxis(ap=yidx[:, r:r + 1].bitcast(U32), axis=0),
                                        yt[:, r, :], None, bounds_check=TOK - 1, oob_is_err=False).then_inc(d_out[r], 16)

            pipeline(pool, ROUTED, RING, 2, [(2, r_lo), (4, r_scatter)])

        @block.vector
        def _(dve):
            v = nc.vector
            steps = [0]

            def then(ins):
                steps[0] += 1
                ins.then_inc(dv, 1)
                dve.wait_ge(dv, steps[0])

            def split_low(g, r):
                row = lambda a: a[:, bass.ds(2 * g + r, 1), :].rearrange("p o c -> p (o c)")
                dve.wait_ge(w_split_hi, 2 * g + r + 1)
                v.scalar_tensor_tensor(row(wlo), wraw[:, r, :], WS, row(whi), ALU.mult, ALU.subtract).then_inc(w_split, 1)

            for q in range(NQ):
                dve.wait_ge(x_in[q], 16)
                for t in range(NT // NQ * q, NT // NQ * (q + 1)):
                    ins = v.bn_stats(stats[:, t, :], base[:, t, :])
                ins.then_inc(stats_done, 1)
            dve.wait_ge(stats_done, NQ)
            half = lambda k: stats[:, :, k]
            v.tensor_tensor(st[:, 0, :], half(1), half(4), ALU.add)
            v.tensor_tensor(st[:, 2, :], half(2), half(5), ALU.add)
            then(v.tensor_tensor(st[:, 1, :], half(1), half(4), ALU.subtract))
            then(v.scalar_tensor_tensor(st[:, 3, :], st[:, 1, :], P / 4.0, st[:, 1, :], ALU.mult, ALU.mult))
            then(v.tensor_tensor(st[:, 2, :], st[:, 2, :], st[:, 3, :], ALU.add))
            v.tensor_scalar(st[:, 4, :], st[:, 2, :], 1.0 / P, EPS, ALU.mult, ALU.add).then_inc(var_ready, 1)
            then(v.tensor_scalar(st[:, 0, :], st[:, 0, :], 0.5, None, ALU.mult))
            dve.wait_ge(csum_done, 1)
            then(v.tensor_scalar(csum[:], pY[:, 1, 0:P], 1 / XS, None, ALU.mult))
            dve.wait_ge(wp_hi, 1)
            v.scalar_tensor_tensor(wp[:, 1, :], wp_raw[:], WS, wp[:, 0, :], ALU.mult, ALU.subtract).then_inc(small_split, 1)
            dve.wait_ge(wp_hi, 2)
            v.scalar_tensor_tensor(bo[0:1, 1, :], bo_raw[:], WS, bo[0:1, 0, :], ALU.mult, ALU.subtract).then_inc(small_split, 1)

            dve.wait_ge(root_ready, 1)
            then(v.reciprocal(st[:, 6, :], st[:, 5, :]))
            then(v.tensor_tensor(st[:, 6, :], st[:, 6, :], st[:, 4, :], ALU.mult))
            then(v.tensor_tensor(st[:, 6, :], st[:, 6, :], st[:, 5, :], ALU.add))
            then(v.reciprocal(st[:, 7, :], st[:, 6, :]))
            then(v.tensor_scalar(st[:, 7, :], st[:, 7, :], 2 * XS, None, ALU.mult))

            def normalise(g, r):
                i = 4 * g + r
                if past(i, 4):
                    dve.wait_ge(rows_lo, i - 3)
                for j in range(TPB):
                    t = TPB * i + j
                    ins = v.tensor_scalar(xs[:, r, j, :], base[:, bass.ds(t, 1), :].rearrange("p o c -> p (o c)"),
                                          st[:, 0, bass.ds(t, 1)], st[:, 7, bass.ds(t, 1)], ALU.subtract, ALU.mult)
                ins.then_inc(xs_ready, 1)

            def read_projections(g, r):
                i = 4 * g + r
                dve.wait_ge(proj_done, i + 1)
                v.scalar_tensor_tensor(proj[:, bass.ds(TPB * i, TPB), :],
                                       pV[:, r % 2, 0:TPB * PROJ].rearrange("p (j c) -> p j c", c=PROJ), 1 / (XS * WS),
                                       bp[:].unsqueeze(1).broadcast_to([P, TPB, PROJ]),
                                       ALU.mult, ALU.add).then_inc(proj_read, 1)

            pipeline(dve, NB, 4, 4, [(0, normalise), (3, read_projections)])
            for r in range(NSH):
                split_low(0, r)
            dve.wait_ge(proj_read, NB)

            logits = proj[:, :, 2 * HP:PROJ]
            wide8 = lambda a: a.unsqueeze(2).broadcast_to([P, NT, E])
            from_last = c["from_last"][:].unsqueeze(1).broadcast_to([P, NT, E])

            def largest(values, eq, score, out_max, out_rank):
                then(v.tensor_reduce(out_max, values, AX.X, ALU.max))
                then(v.tensor_tensor(eq, values, wide8(out_max), ALU.is_equal))
                then(v.tensor_tensor(score, eq, from_last, ALU.mult))
                then(v.tensor_reduce(out_rank, score, AX.X, ALU.max))

            largest(logits, r8[:, 0], r8[:, 1], rt[:, 0, :], rt[:, 1, :])
            then(v.tensor_tensor(r8[:, 2], r8[:, 1], wide8(rt[:, 1, :]), ALU.is_equal))
            then(v.scalar_tensor_tensor(r8[:, 3], r8[:, 2], -1e30, logits, ALU.mult, ALU.add))
            largest(r8[:, 3], r8[:, 0], r8[:, 1], rt[:, 2, :], rt[:, 3, :])
            v.tensor_tensor(rt[:, 4, :], rt[:, 2, :], rt[:, 0, :], ALU.subtract).then_inc(gap_ready, 1)
            then(v.tensor_tensor(rt[:, 6, :], rt[:, 1, :], rt[:, 3, :], ALU.max))
            then(v.tensor_tensor(rt[:, 7, :], rt[:, 1, :], rt[:, 3, :], ALU.min))
            then(v.tensor_scalar(rt[:, 8, :], rt[:, 6, :], -1.0, float(E), ALU.mult, ALU.add))
            then(v.tensor_scalar(rt[:, 9, :], rt[:, 6, :], 0.5, 2.5, ALU.mult, ALU.add))
            then(v.tensor_tensor(rt[:, 8, :], rt[:, 8, :], rt[:, 9, :], ALU.mult))
            then(v.tensor_tensor(rt[:, 8, :], rt[:, 8, :], rt[:, 7, :], ALU.subtract))
            then(v.tensor_scalar(pair16[:], rt[:, 8, :], E - 1.0, None, ALU.add))

            scan, place = scratch_a[:, 0:NPAIR * NT], scratch_b[:, 0:NPAIR * NT]
            scan3, place3 = (a.rearrange("p (q t) -> p q t", q=NPAIR) for a in (scan, place))
            then(v.tensor_tensor(member, pair16[:].unsqueeze(1).broadcast_to([P, NPAIR, NT]),
                                 c["pair_ids"].rearrange("p (q t) -> p q t", q=NPAIR), ALU.is_equal))
            then(v.tensor_tensor_scan(scan, member_row, member_row, 0.0, ALU.add, ALU.max))
            then(v.memset(seg[:, 0, :], 0.0))
            then(v.tensor_copy(seg[:, 0, 1:NPAIR], scan3[:, 0:NPAIR - 1, NT - 1]))
            v.tensor_tensor(seg16[:], scan3[:, :, NT - 1], seg[:, 0, :], ALU.subtract).then_inc(seg_ready, 1)
            dve.wait_ge(gap_exp, 1)
            then(v.tensor_scalar(rt[:, 6, :], rt[:, 5, :], 1.0, None, ALU.add))
            then(v.reciprocal(rt[:, 7, :], rt[:, 6, :]))
            then(v.tensor_scalar(rt[:, 7, :], rt[:, 7, :], 1 / (XS * WS), None, ALU.mult))
            then(v.tensor_tensor(rt[:, 8, :], rt[:, 7, :], rt[:, 5, :], ALU.mult))
            then(v.tensor_tensor(rt[:, 9, :], rt[:, 7, :], rt[:, 8, :], ALU.subtract))
            then(v.tensor_tensor(rt[:, 10, :], rt[:, 1, :], rt[:, 3, :], ALU.is_gt))
            then(v.tensor_tensor(rt[:, 9, :], rt[:, 9, :], rt[:, 10, :], ALU.mult))
            dve.wait_ge(meta_init, 2)
            then(v.tensor_tensor(rows32[:, :, CWA], rt[:, 8, :], rt[:, 9, :], ALU.add))
            v.tensor_tensor(rows32[:, :, CWB], rt[:, 7, :], rt[:, 9, :], ALU.subtract).then_inc(cw_ready, 1)
            dve.wait_ge(seg_done, 1)
            then(v.tensor_scalar(segi[:, 0, :], pY[:, 0, 32:32 + NPAIR], P - 1.0, None, ALU.add))
            then(v.tensor_scalar(segi[:, 1, :], segi[:, 0, :], 7, None, ALU.logical_shift_right))
            then(v.tensor_copy(seg[:, 1, :], segi[:, 1, :]))
            then(v.tensor_tensor_scan(seg[:, 2, :], seg[:, 1, :], seg[:, 1, :], 0.0, ALU.add, ALU.max))
            then(v.tensor_tensor(seg[:, 3, :], seg[:, 2, :], seg[:, 1, :], ALU.subtract))
            then(v.scalar_tensor_tensor(seg[:, 4, :], seg[:, 3, :], float(P), pY[:, 0, 0:NPAIR], ALU.mult, ALU.add))
            then(v.scalar_tensor_tensor(seg[:, 5, :], seg[:, 4, :], -1.0, seg[:, 0, :], ALU.add, ALU.subtract))
            then(v.tensor_tensor(place3, scan3, seg[:, 5, :].unsqueeze(2).broadcast_to([P, NPAIR, NT]), ALU.add))
            then(v.tensor_tensor(place, place, member_row, ALU.mult))
            then(v.tensor_reduce(rt[:, 11, :], place3.rearrange("p q t -> p t q"), AX.X, ALU.add))
            v.tensor_copy(slot[:], rt[:, 11, :]).then_inc(slot_ready, 1)

            then(v.tensor_scalar(tab_scr[:, 0, :], seg[:, 3, :], c["part"][:], None, ALU.is_le))
            for k, name in enumerate(("pair_step_a", "pair_step_b")):
                then(v.tensor_tensor_reduce(tab_scr[:, 1, :], tab_scr[:, 0, :], c[name][:], 1.0, 0.0,
                                            ALU.mult, ALU.add, tab_f[:, k:k + 1]))
            v.tensor_copy(tab16[:], tab_f[:]).then_inc(tab_ready, 1)

            att = proj[:, :, HP:2 * HP].rearrange("p t (h k) -> p t h k", k=POINTS)
            weight4 = weight[:].rearrange("p (t h k) -> p t h k", h=HEADS, k=POINTS)
            weight3 = weight[:].rearrange("p (g k) -> p g k", k=POINTS)
            then(v.tensor_reduce(wmax[:, 0, :].rearrange("p (t h) -> p t h", h=HEADS), att, AX.X, ALU.max))
            v.tensor_tensor(weight4, att, wmax[:, 0, :].rearrange("p (t h) -> p t h", h=HEADS).unsqueeze(3)
                            .broadcast_to([P, NT, HEADS, POINTS]), ALU.subtract).then_inc(logit_ready, 1)
            dve.wait_ge(tab_done, 1)
            v.tensor_scalar(experts[:].rearrange("p t k -> p k t"), pY[0:1, 0, P:3 * P].rearrange("p (k t) -> p k t", k=2), float(NSH), None,
                            ALU.add).then_inc(experts_ready, 1)

            clipped, size = scratch_a, scratch_b
            whole = free_lo[:, 0:NT * HP].bitcast(I32)
            then(v.tensor_scalar(clipped.rearrange("p (t k) -> p t k", k=HP), proj[:, :, 0:HP], 127.5, -128.0,
                                 ALU.min, ALU.max))
            then(v.scalar_tensor_tensor(size, clipped, -1.0, clipped, ALU.mult, ALU.max))
            then(v.tensor_copy(whole, size))
            then(v.scalar_tensor_tensor(fl16[0], whole, 0.0, size, ALU.add, ALU.is_gt))
            then(v.tensor_tensor(fl16[1], whole, fl16[0], ALU.subtract))
            then(v.tensor_scalar(fl16[0], fl16[1], -2.0, float(P), ALU.mult, ALU.add))
            then(v.scalar_tensor_tensor(fl16[0], clipped, 0.0, fl16[0], ALU.is_lt, ALU.mult))
            then(v.tensor_tensor(idx, fl16[1], fl16[0], ALU.add))
            then(v.tensor_scalar(ilo[:], idx, LO16 - 1, None, ALU.bitwise_and))
            then(v.tensor_scalar(ihi[:], idx, 4, HI16 - 1, ALU.logical_shift_right, ALU.bitwise_and))

            dve.wait_ge(logit_exp, 1)
            then(v.tensor_reduce(wmax[:, 1, :], weight3, AX.X, ALU.add))
            then(v.reciprocal(wmax[:, 0, :], wmax[:, 1, :]))
            then(v.tensor_tensor(weight3, weight3, wmax[:, 0, :].unsqueeze(2).broadcast_to([P, NT * HEADS, POINTS]),
                                 ALU.mult))
            v.memset(seg[:, 0, 0:1], 0.0).then_inc(scratch_free, 1)

            first_row = xT[:, 0:NB:2, :, 0].unsqueeze(3).broadcast_to([P, BATCH, 2, HI16 * GRP])
            mask = c["high_mask"][:].unsqueeze(1).unsqueeze(1).broadcast_to([P, BATCH, 2, HI16 * GRP])
            dve.wait_ge(xt_ready, NB)
            v.tensor_tensor(tsel.rearrange("p (b s) c -> p b s c", s=2), mask, first_row, ALU.mult).then_inc(tsel_ready, 1)
            with dve.Fori(1, NE // 2) as g:
                for r in range(2):
                    split_low(g, r)
            dve.wait_ge(table_done, 1)
            same = c["same_gather"][:].unsqueeze(1).broadcast_to([P, 8, HI16 * GRP])
            for k in range(2):
                ins = v.tensor_tensor(table[:, 4 * k:4 * k + 4].rearrange("p b s c -> p (b s) c"),
                                      pV[:, k, :].rearrange("p (g c) -> p g c", g=8), same, ALU.mult)
            ins.then_inc(table_ready, 1)

            def one_hots(b, u):
                if u:
                    return
                seg32 = lambda a: a[:, bass.ds(8 * HP * b, 8 * HP)].rearrange("p (g h) -> p g h", h=GRP)
                if past(8 * b, 1):
                    dve.wait_ge(v_done, 4 * b)
                for k in range(LO16):
                    ins = v.tensor_scalar(hot[:, :, k, :], seg32(ilo), float(k), None, ALU.is_equal)
                ins.then_inc(hot_ready, 1)
                for k in range(HI16):
                    ins = v.scalar_tensor_tensor(aw[:, :, k, :], seg32(ihi), float(k), seg32(weight),
                                                 ALU.is_equal, ALU.mult)
                ins.then_inc(aw_ready, 1)

            def hf_unit(b, u):
                n = 8 * b + u
                dve.wait_ge(silu_done, n + 1)
                if past(n, 2):
                    dve.wait_ge(lo_done, n - 1)
                v.scalar_tensor_tensor(hf[:, u % 2, :], pB[:, u % 2, :], 1 / (XS * WS), silu[:, u % 2, :],
                                       ALU.mult, ALU.mult).then_inc(hf_done, 1)

            def weigh(b, u):
                if u % 2 == 0:
                    return
                r = u // 2
                if r == 0:
                    dve.wait_ge(aw_ready, b + 1)
                    if past(8 * b, 1):
                        dve.wait_ge(attn_added, b)
                dve.wait_ge(v_done, 4 * b + r + 1)
                for t in range(2):
                    k = 2 * r + t
                    ins = v.tensor_tensor_reduce(vscr[:, t, :], pV[:, 1, t * 256:(t + 1) * 256],
                                                 aw[:, NG * k:NG * (k + 1), :, :].rearrange("p g a h -> p (g a h)"),
                                                 1.0, 0.0, ALU.mult, ALU.add, attn[:, k:k + 1])
                ins.then_inc(v_read, 1)

            def add_shared(b, u):
                if u % 4 != 3:
                    return
                i = 2 * b + u // 4
                dve.wait_ge(l2, 4 * i + 4)
                if u == 7:
                    dve.wait_ge(attn_added, b + 1)
                row = base_blk[:, bass.ds(i, 1), :].rearrange("p o w -> p (o w)")
                v.scalar_tensor_tensor(row, pY[:, u // 4, :], 1 / WS, row, ALU.mult, ALU.add).then_inc(y_read, 1)

            def add_attention(b, u):
                if u != 7:
                    return
                dve.wait_ge(v_read, 4 * b + 4)
                dve.wait_ge(y_read, 2 * b + 1)
                for k in range(8):
                    row = base[:, bass.ds(8 * b + k, 1), :].rearrange("p o c -> p (o c)")
                    ins = v.scalar_tensor_tensor(row, csum[:], attn[:, k:k + 1], row, ALU.mult, ALU.add)
                ins.then_inc(attn_added, 1)

            pipeline(dve, 4 * NB, 8, 1, [(0, one_hots), (0, hf_unit), (0, weigh), (2, add_shared), (0, add_attention)])

            dve.wait_ge(lo_done, 4 * NB)

            def r_meta(g, r):
                dve.wait_ge(d_in[r], 16 * (g + 1))
                if past(RING * g + r, RING):
                    dve.wait_ge(d_y, RING * g + r - RING + 1)
                v.tensor_copy(meta[:, r, :], xr[:, r, CWA:CWA + 4]).then_inc(d_meta, 1)

            def r_hf(g, r):
                t = RING * g + r
                dve.wait_ge(d_meta, t + 1)
                dve.wait_ge(d_silu, t + 1)
                for k in range(2):
                    ins = v.scalar_tensor_tensor(hf[:, r % 2, k * HID:(k + 1) * HID],
                                                 pAB[:, 2 * (r % 2) + k, HID:2 * HID], meta32[:, r, k:k + 1],
                                                 silu[:, r % 2, k * HID:(k + 1) * HID], ALU.mult, ALU.mult)
                ins.then_inc(d_hf, 1)

            def r_hT_lo(g, r):
                t = RING * g + r
                dve.wait_ge(d_hturn, t + 1)
                v.tensor_copy(h_lo[:, 2 + r % 2, :], pY16[:, 1, 0:512]).then_inc(d_hT_lo, 1)

            def r_y(g, r):
                t = RING * g + r
                dve.wait_ge(d_l2, t + 1)
                if past(t, RING):
                    dve.wait_ge(d_out[r], 16 * g)
                v.tensor_reduce(yt[:, r, :], pS.rearrange("p (s c) -> p c s", s=2), AX.X, ALU.add)
                v.tensor_copy(yidx[:, r:r + 1], meta[:, r, 2:3]).then_inc(d_y, 1)

            pipeline(dve, ROUTED, RING, 2, [(2, r_hf), (4, r_y), (3, r_hT_lo), (0, r_meta)])

            dve.wait_ge(attn_added, BATCH)
            dve.wait_ge(y_read, NB)
            with dve.Fori(0, NB // 4) as q:
                for r in range(4):
                    dve.wait_ge(y_in[r], 16 * (q + 1))
                    tiles = base[:, bass.ds(4 * (4 * q + r), TPB), :]
                    v.scalar_tensor_tensor(tiles, y_all[:, bass.ds(4 * (4 * q + r), TPB), :], 1 / WS, tiles,
                                           ALU.mult, ALU.add).then_inc(fin, 1)


def kernel(**inputs):
    import concourse.bacc as _bacc
    from concourse.bass_utils import run_bass_kernel_spmd as _run

    a = {k.replace("L0_attn_", "").replace("L0_ffn_", "f_"): np.asarray(v) for k, v in inputs.items()}
    wproj = np.concatenate([a["W_off"][:, 0::2], a["W_attn"], a["f_router_w"].T], axis=1)
    bproj = np.concatenate([a["b_off"][0::2], a["b_attn"], a["f_expert_bias"]])
    w1 = np.concatenate([a["f_sw1"], a["f_w1"]])
    w3 = np.concatenate([a["f_sw3"], a["f_w3"]])
    w2 = np.concatenate([a["f_sw2"], a["f_w2"]])
    by_half = w2.transpose(0, 2, 1).reshape(NE, HID // P, P, P).transpose(0, 2, 1, 3).reshape(NE, P, HID)
    wall = np.concatenate([w1.transpose(0, 2, 1), w3.transpose(0, 2, 1), by_half], axis=2)
    const = constants()
    arrays = {
        "x": a["x"], "wall": wall, "wproj": wproj, "bproj": np.broadcast_to(bproj[None, :], (P, PROJ)),
        "w_out": a["W_out"], "b_out": a["b_out"][None, :],
    }
    arrays = {k: np.ascontiguousarray(v) for k, v in arrays.items()}
    arrays |= {"c_" + k: np.ascontiguousarray(v) for k, v in const.items()}

    nc = _bacc.Bacc("TRN2", target_bir_lowering=False, num_devices=1)
    dram = {k: nc.dram_tensor("in_" + k, v.shape, mybir.dt.from_np(v.dtype), kind="ExternalInput").ap()
            for k, v in arrays.items()}
    out = nc.dram_tensor("out_dram", a["x"].shape, F32, kind="ExternalOutput").ap()
    sorted_rows = nc.dram_tensor("sorted_rows", [SLOTS, ROWW], I32, kind="Internal").ap()
    y_rows = nc.dram_tensor("y_rows", [TOK, P], F32, kind="Internal").ap()
    consts = {k: dram["c_" + k] for k in const}
    layer_kernel(nc, dram["x"], dram["wall"], dram["wproj"], dram["bproj"], dram["w_out"], dram["b_out"],
                 consts, out, sorted_rows, y_rows)
    got = _run(nc, [{"in_" + k: v for k, v in arrays.items()}], core_ids=[0])
    return got.results[0]["out_dram"]
```

```python
from contextlib import ExitStack

import numpy as np

import concourse.bass as bass
from concourse import mybir

ALU = mybir.AluOpType
ACT = mybir.ActivationFunctionType
AX = mybir.AxisListType
F32 = mybir.dt.float32
F16 = mybir.dt.float16
I32 = mybir.dt.int32
I16 = mybir.dt.int16
U32 = mybir.dt.uint32

P = 128
BATCH, SEQ = 8, 1024
TOK = BATCH * SEQ
NT = TOK // P
BLK = 512
TPB = BLK // P
NB = TOK // BLK
HEADS, POINTS = 8, 4
HP = HEADS * POINTS
E, NSH, HID = 8, 2, 256
NE = E + NSH
NPAIR = E * (E - 1) // 2
PROJ = 2 * HP + E
NQ = 4
RING = 4
ROUTED = -(-((TOK + NPAIR * (P - 1)) // P) // RING) * RING
SLOTS = ROUTED * P
ROWW = 132
CWA, CWB, TOKW = 128, 129, 130
XS = 4096.0
WS = 64.0
EPS = 1e-5
LO16, HI16 = 16, 8
GRP = 8
NG = HP // GRP
W1, W3, W2 = 0, HID, 2 * HID
WCOL = 3 * HID
UNITS = TOK // BLK * NSH * 2
ROUND = 8
ATT = 4
APAIRS = NT // 2
GAP_UNIT, SEG_UNIT, TAB_UNIT, TABLE_UNIT, LOGIT_UNIT, SCATTER_UNIT = 3, 7, 12, 14, 14, 12


def constants():
    p = np.arange(P)
    b_of, h_of = p // GRP, p % GRP
    ah = np.arange(HI16 * GRP)
    a_of, g_of = ah // GRP, ah % GRP
    ea, eb = np.array([(a, b) for a in range(E) for b in range(a + 1, E)]).T
    token = (np.arange(NT)[None, :] // TPB) * BLK + p[:, None] * TPB + np.arange(NT)[None, :] % TPB
    pad = np.zeros((P, ROWW), np.int32)
    pad[:, TOKW] = TOK + p
    f16, f32 = np.float16, np.float32
    wide = lambda v: np.broadcast_to(v[None, :], (P, len(v)))
    return {
        "ident": np.eye(P, dtype=f16),
        "before": (p[:, None] < p[None, :]).astype(f16),
        "ones": np.ones((P, P), f16),
        "low_sel": (p[:, None] % LO16 == b_of[None, :]).astype(f16),
        "high_mask": (p[:, None] // LO16 == a_of[None, :]).astype(f16),
        "same_gather": (h_of[:, None] == g_of[None, :]).astype(f16),
        "pair_ids": wide(np.repeat(np.arange(NPAIR), NT)).astype(f16),
        "pair_step_a": wide(np.diff(ea, prepend=0)).astype(f32),
        "pair_step_b": wide(np.diff(eb, prepend=0)).astype(f32),
        "from_last": wide(E - np.arange(E)).astype(f32),
        "part": p[:, None].astype(f32),
        "token": token.astype(np.int32),
        "pad_row": pad,
        "ones32": np.ones((P, P), f32),
    }


def past(t, k):
    return not isinstance(t, int) or t >= k


def pipeline(eng, total, unroll, peel, parts, begin=lambda g: None):
    last = max(lag for lag, _ in parts)
    for s in range(unroll * peel):
        if s % unroll == 0:
            begin(s // unroll)
        for lag, part in parts:
            if s >= lag:
                part((s - lag) // unroll, (s - lag) % unroll)
    if peel < total // unroll:
        with eng.Fori(peel, total // unroll) as g:
            begin(g)
            for r in range(unroll):
                for lag, part in parts:
                    part(g + (r - lag) // unroll, (r - lag) % unroll)
    for s in range(total, total + last):
        if s % unroll == 0:
            begin(s // unroll)
        for lag, part in parts:
            if s - lag < total:
                part((s - lag) // unroll, (s - lag) % unroll)


def straight(lo, hi, parts):
    for s in range(lo, hi):
        for lag, part, first, last in parts:
            if first <= s - lag < last:
                part((s - lag) // ROUND, (s - lag) % ROUND)


def rounds(eng, lo, hi, parts):
    with eng.Fori(lo, hi) as g:
        for u in range(ROUND):
            for lag, part, _, _ in parts:
                part(g + (u - lag) // ROUND, (u - lag) % ROUND)


def layer_kernel(nc, x, wall, wproj, bproj, w_out, b_out, const, out, sorted_rows, y_rows):
    with ExitStack() as ctx:
        def sb(name, shape, dt):
            return ctx.enter_context(nc.sbuf_tensor(name, shape, dt))

        def sem(name):
            return ctx.enter_context(nc.semaphore(name))

        pAB = ctx.enter_context(nc.psum_tensor("pAB", [P, 4, 512], F32))
        pA, pB = pAB[:, 0:2, :], pAB[:, 2:4, :]
        pY = ctx.enter_context(nc.psum_tensor("pY", [P, 2, 512], F32))
        pV = ctx.enter_context(nc.psum_tensor("pV", [P, 2, 512], F32))

        base = sb("base", [P, NT, P], F32)
        rows = sb("rows", [P, NT, ROWW], I32)
        xT = sb("xT", [P, NB, 2, BLK], F16)
        wsp = sb("wsp", [P, 2, NE, WCOL], F16)
        whi, wlo = wsp[:, 0], wsp[:, 1]
        wraw = sb("wraw", [P, 2, WCOL], F32)
        proj = sb("proj", [P, NT, PROJ], F32)
        wp_raw = sb("wp_raw", [P, PROJ], F32)
        wp = sb("wp", [P, 2, PROJ], F16)
        bp = sb("bp", [P, PROJ], F32)
        wo = sb("wo", [P, P], F32)
        csum = sb("csum", [P, P], F32)
        bo_raw = sb("bo_raw", [1, P], F32)
        bo = sb("bo", [P, 2, P], F16)
        units = sb("units", [P, 4, 512], F32)
        silu, hf = units[:, 0:2, :], units[:, 2:4, :]
        xs = units[:].rearrange("p r (j c) -> p r j c", j=TPB)
        h_hi = sb("h_hi", [P, 4, 512], F16)
        h_lo = sb("h_lo", [P, 4, 512], F16)
        c = {}
        hotT = sb("hotT", [P, 2, 8 * P], F16)
        for name, a in const.items():
            c[name] = (hotT[:].rearrange("p r c -> p (r c)")[:, 0:NPAIR * NT] if name == "pair_ids"
                       else sb("c_" + name, list(a.shape), a.dtype))
        stats = sb("stats", [P, NT, 6], F32)
        st = sb("st", [P, 8, NT], F32)
        rt = sb("rt", [P, 12, NT], F32)
        free_hi = whi[:, NSH:, :].rearrange("p e c -> p (e c)").bitcast(F32)
        free_lo = wlo[:, NSH:, :].rearrange("p e c -> p (e c)").bitcast(F32)
        r8 = free_hi[:, 0:4 * NT * E].rearrange("p (k t e) -> p k t e", k=4, t=NT)
        scratch_a = free_lo[:, 0:NT * HP]
        scratch_b = free_hi[:, 0:NT * HP]
        member_row = free_lo[:, NT * HP:].bitcast(F16)[:, 0:NPAIR * NT]
        member = member_row.rearrange("p (q t) -> p q t", q=NPAIR)
        pair16 = sb("pair16", [P, NT], F16)
        seg = sb("seg", [P, 8, NPAIR], F32)
        seg16 = sb("seg16", [P, NPAIR], F16)
        segi = sb("segi", [P, 2, NPAIR], I32)
        slot = sb("slot", [P, NT], I32)
        tab16 = sb("tab16", [P, 2], F16)
        tab_scr = sb("tab_scr", [P, 2, NPAIR], F32)
        tab_f = sb("tab_f", [P, 2], F32)
        experts = sb("experts", [1, P, 2], I32)
        hot = sb("hot", [P, 2, TPB, NG, LO16, GRP], F16)
        aw = sb("aw", [P, 2, TPB, NG, HI16, GRP], F32)
        hot_row, aw_row = (a[:].rearrange("p s t g b h -> p (s t g b h)") for a in (hot, aw))
        wmax = aw_row[:, 0:2 * NT * HEADS].rearrange("p (k t h) -> p k t h", k=2, h=HEADS)
        fl16 = [free_hi[:, NT * HP:].bitcast(F16), hot_row[:, 0:NT * HP]]
        idx = free_lo[:, NT * HP:].bitcast(I16)
        offsets = proj[:, :, 0:HP]
        weight = proj[:, :, HP:2 * HP]
        proj_i16 = proj[:].bitcast(I16)
        ilo, ihi = proj_i16[:, :, 0:HP], proj_i16[:, :, HP:2 * HP]
        table = sb("table", [P, BATCH, 2, HI16 * GRP], F16)
        attn = sb("attn", [P, 2, 8], F32)
        attn_all = sb("attn_all", [P, NT], F32)
        xr = (wraw[:].rearrange("p r c -> p (r c)")[:, 0:RING * ROWW].bitcast(I32)
              .rearrange("p (r w) -> p r w", r=RING))
        meta = sb("meta", [P, RING, 4], I32)
        xrT = xT[:, 0].rearrange("p s (r c) -> p (s r) c", c=2 * P)
        yt = sb("yt", [P, RING, P], F32)
        vscr = yt[:].rearrange("p (t r) c -> p t (r c)", t=2)
        tsel = yt[:].rearrange("p r c -> p (r c)").bitcast(F16).rearrange("p (g c) -> p g c", g=BATCH * 2)
        yidx = sb("yidx", [P, RING], I32)

        y_all = rows[:, :, 0:P].bitcast(F32)
        rows16 = rows[:].bitcast(F16)
        rows32 = rows[:].bitcast(F32)
        xr16 = xr.bitcast(F16)
        meta32 = meta[:].bitcast(F32)
        pY16, pV16 = pY[:].bitcast(F16), pV[:].bitcast(F16)
        pT16 = pV16[:, 0, 0:2 * P]
        pS = pV[:, 1, 0:2 * P]

        x_in = [sem(f"x_in{q}") for q in range(NQ)]
        w_in = [sem("w_in0"), sem("w_in1")]
        const_in = sem("const_in")
        pad_out = sem("pad_out")
        w_split_hi = sem("w_split_hi")
        w_split = sem("w_split")
        wp_hi = sem("wp_hi")
        small_split = sem("small_split")
        pool_go = sem("pool_go")
        bo_zero = sem("bo_zero")
        stats_done = sem("stats_done")
        dv = sem("dv")
        var_ready = sem("var_ready")
        root_ready = sem("root_ready")
        xs_ready = sem("xs_ready")
        rows_hi = sem("rows_hi")
        rows_lo = sem("rows_lo")
        turned = sem("turned")
        xt_ready = sem("xt_ready")
        proj_done = sem("proj_done")
        proj_read = sem("proj_read")
        meta_init = sem("meta_init")
        scratch_free = sem("scratch_free")
        gap_ready = sem("gap_ready")
        gap_exp = sem("gap_exp")
        cw_ready = sem("cw_ready")
        seg_ready = sem("seg_ready")
        seg_done = sem("seg_done")
        slot_ready = sem("slot_ready")
        tab_ready = sem("tab_ready")
        tab_done = sem("tab_done")
        experts_ready = sem("experts_ready")
        logit_ready = sem("logit_ready")
        logit_exp = sem("logit_exp")
        tsel_ready = sem("tsel_ready")
        table_done = sem("table_done")
        table_ready = sem("table_ready")
        csum_done = sem("csum_done")
        sorted_in = sem("sorted_in")
        l1 = sem("l1")
        silu_done = sem("silu_done")
        hf_done = sem("hf_done")
        hi_done = sem("hi_done")
        lo_done = sem("lo_done")
        l2 = sem("l2")
        y_read = sem("y_read")
        hot_ready = sem("hot_ready")
        aw_ready = sem("aw_ready")
        hot_turned = sem("hot_turned")
        hotT_ready = sem("hotT_ready")
        v_done = sem("v_done")
        v_read = sem("v_read")
        attn_saved = sem("attn_saved")
        attn_added = sem("attn_added")
        d_in = [sem(f"d_in{r}") for r in range(RING)]
        d_turn = sem("d_turn")
        d_meta = sem("d_meta")
        d_xt = sem("d_xt")
        d_l1 = sem("d_l1")
        d_silu = sem("d_silu")
        d_hf = sem("d_hf")
        d_hi = sem("d_hi")
        d_lo = sem("d_lo")
        d_hturn = sem("d_hturn")
        d_hT_hi = sem("d_hT_hi")
        d_hT_lo = sem("d_hT_lo")
        d_l2 = sem("d_l2")
        d_y = sem("d_y")
        d_out = [sem(f"d_out{r}") for r in range(RING)]
        y_in = [sem(f"y_in{r}") for r in range(4)]
        fin = sem("fin")
        out_done = sem("out_done")

        n_const = len(const) + 4
        x_blk = x.rearrange("b (k p j) c -> (b k) p (j c)", p=P, j=TPB)
        out_blk = out.rearrange("b (k p j) c -> (b k) p (j c)", p=P, j=TPB)
        base_blk = base[:].rearrange("p (i j) c -> p i (j c)", j=TPB)
        sorted_tiles = sorted_rows.rearrange("(t p) w -> t p w", p=P)
        y_blk = y_rows.rearrange("(i p j) c -> i p j c", p=P, j=TPB)

        block = ctx.enter_context(nc.Block())

        @block.sync
        def _(sp):
            for q in range(NQ):
                sp.dma_start(base_blk[:, NB // NQ * q:NB // NQ * (q + 1), :],
                             x_blk[NB // NQ * q:NB // NQ * (q + 1)].rearrange("i p w -> p i w")).then_inc(x_in[q], 16)
            sp.wait_ge(const_in, 16 * n_const)
            sp.dma_start(sorted_rows.rearrange("(t p) w -> p t w", p=P),
                         c["pad_row"][:].unsqueeze(1).broadcast_to([P, ROUTED, ROWW])).then_inc(pad_out, 16)

            with sp.Fori(1, NE // 2) as g:
                for r in range(2):
                    sp.wait_ge(w_split, 2 * g + r - 1)
                    sp.dma_start(wraw[:, r, :], wall[bass.ds(2 * g + r, 1)].rearrange("o p w -> p (o w)")
                                 ).then_inc(w_in[r], 16)

            sp.wait_ge(w_split, NE)
            sp.wait_ge(sorted_in, 16 * NT)
            for r in range(RING):
                sp.dma_start(xr[:, r, :], sorted_tiles[r]).then_inc(d_in[r], 16)
            with sp.Fori(1, ROUTED // RING) as g:
                for r in range(RING):
                    sp.wait_ge(d_turn, RING * g + (r + 1 - RING))
                    sp.wait_ge(d_meta, RING * g + (r + 1 - RING))
                    sp.dma_start(xr[:, r, :], sorted_tiles[bass.ds(RING * g + r, 1)].rearrange("o p w -> p (o w)")
                                 ).then_inc(d_in[r], 16)

            for r in range(RING):
                sp.wait_ge(d_out[r], 16 * (ROUTED // RING))
            for r in range(4):
                sp.dma_start(y_all[:, TPB * r:TPB * r + TPB, :], y_blk[r]).then_inc(y_in[r], 16)
            with sp.Fori(1, NB // 4) as q:
                for r in range(4):
                    sp.wait_ge(y_in[r], 16 * q)
                    sp.dma_start(y_all[:, bass.ds(16 * q + 4 * r, TPB), :],
                                 y_blk[bass.ds(4 * q + r, 1)].rearrange("o p j c -> p (o j) c")).then_inc(y_in[r], 16)

        @block.tensor
        def _(pe):
            pe.wait_ge(const_in, 16 * n_const)
            pe.matmul(pY[:, 1, 0:P], c["ones32"][:], wo[:], start=True, stop=True).then_inc(csum_done, 1)

            def turn(g, r):
                i = 4 * g + r
                pe.wait_ge(rows_lo, i + 1)
                if past(i, 2):
                    pe.wait_ge(xt_ready, i - 1)
                for bank, off in ((pA, 0), (pB, P)):
                    for j in range(TPB):
                        mm = pe.matmul(bank[:, r % 2, j * P:(j + 1) * P],
                                       rows16[:, bass.ds(TPB * i + j, 1), off:off + P].rearrange("p o c -> p (o c)"),
                                       c["ident"][:], start=True, stop=True)
                mm.then_inc(turned, 1)

            def project(g, r):
                i = 4 * g + r
                pe.wait_ge(xt_ready, i + 1)
                if past(i, 2):
                    pe.wait_ge(proj_read, i - 1)
                for j in range(TPB):
                    for m, (s, w) in enumerate(((0, 0), (0, 1), (1, 0), (1, 1))):
                        mm = pe.matmul(pV[:, r % 2, j * PROJ:(j + 1) * PROJ],
                                       xT[:, bass.ds(i, 1), s, j * P:(j + 1) * P].rearrange("p o c -> p (o c)"),
                                       wp[:, w, :], start=(m == 0), stop=(m == 3))
                mm.then_inc(proj_done, 1)

            pe.wait_ge(small_split, 1)
            pipeline(pe, NB, 4, 4, [(0, turn), (1, project)])

            def routing_products(g, u):
                n = ROUND * g + u
                if n == SEG_UNIT:
                    pe.wait_ge(seg_ready, 1)
                    pe.matmul(pV[:, 0, 0:NPAIR], c["before"][:], seg16[:], start=True, stop=True)
                    pe.matmul(pV[:, 0, 32:32 + NPAIR], c["ones"][:], seg16[:], start=True, stop=True).then_inc(seg_done, 1)
                if n == TAB_UNIT:
                    pe.wait_ge(tab_ready, 1)
                    for k in range(2):
                        mm = pe.matmul(pV[0:1, 0, (k + 1) * P:(k + 2) * P], tab16[:, k:k + 1], c["ident"][:],
                                       start=True, stop=True)
                    mm.then_inc(tab_done, 1)
                if n == TABLE_UNIT:
                    pe.wait_ge(tsel_ready, 1)
                    for k in range(2):
                        mm = pe.matmul(pV[:, k, :], c["low_sel"][:],
                                       tsel[:, 8 * k:8 * k + 8, :].rearrange("p b c -> p (b c)"), start=True, stop=True)
                    mm.then_inc(table_done, 1)

            def first_products(b, u):
                n, x, h = 8 * b + u, (u // 2) % 2, u % 2
                if past(n, 2):
                    pe.wait_ge(hf_done, n - 1)
                xi = lambda s: xT[:, bass.ds(2 * b + u // 4, 1), s, :].rearrange("p o c -> p (o c)")
                for bank, col in ((pA, W1), (pB, W3)):
                    w = slice(col + h * P, col + (h + 1) * P)
                    pe.matmul(bank[:, u % 2, :], whi[:, x, w], xi(0), start=True, stop=False)
                    pe.matmul(bank[:, u % 2, :], whi[:, x, w], xi(1), start=False, stop=False)
                    mm = pe.matmul(bank[:, u % 2, :], wlo[:, x, w], xi(0), start=False, stop=True)
                mm.then_inc(l1, 1)

            def second_products(b, u):
                n, i, x, h = 8 * b + u, 2 * b + u // 4, (u // 2) % 2, u % 2
                w = slice(W2 + h * P, W2 + (h + 1) * P)
                if u % 4 == 0 and past(i, 2):
                    pe.wait_ge(y_read, i - 1)
                pe.wait_ge(lo_done, n + 1)
                for j in range(TPB):
                    o, t = pY[:, u // 4, j * P:(j + 1) * P], slice(j * P, (j + 1) * P)
                    if u % 4 == 0:
                        pe.matmul(o, c["ones"][:], bo[:, 0, :], start=(j == 0), stop=False, skip_group_check=True)
                        pe.matmul(o, c["ones"][:], bo[:, 1, :], start=False, stop=False, skip_group_check=True)
                    for m, (hid, wt) in enumerate(((h_hi, whi), (h_hi, wlo), (h_lo, whi))):
                        mm = pe.matmul(o, hid[:, u % 4, t], wt[:, x, w], start=False,
                                       stop=(u % 4 == 3 and m == 2), skip_group_check=True)
                mm.then_inc(l2, 1)

            def turn_hot(g, u):
                m = ROUND * (g - ATT) + u
                if u % 2 == 0:
                    pe.wait_ge(hot_ready, (ROUND // 2) * (g - ATT) + (u // 2 + 1))
                if past(m, 1):
                    pe.wait_ge(hotT_ready, m)
                for k in range(2 * NG):
                    mm = pe.transpose(pV16[:, 0, k * P:(k + 1) * P],
                                      hot[:, (u // 2) % 2, 2 * (u % 2) + k // NG, k % NG].rearrange("p b h -> p (b h)"),
                                      c["ident"][:])
                mm.then_inc(hot_turned, 1)

            def pick(g, u):
                m = ROUND * (g - ATT) + u
                pe.wait_ge(hotT_ready, m + 1)
                if past(m, 1):
                    pe.wait_ge(v_read, m)
                for k in range(2 * NG):
                    for s in range(2):
                        mm = pe.matmul(pV[:, 1, k * 64:(k + 1) * 64], hotT[:, u % 2, k * P:(k + 1) * P],
                                       table[:, bass.ds(2 * (g - ATT) + u // 4, 1), s, :].rearrange("p o c -> p (o c)"),
                                       start=(s == 0), stop=(s == 1))
                mm.then_inc(v_done, 1)

            pe.wait_ge(w_split, NSH)
            pe.wait_ge(small_split, 2)
            shared = [(0, first_products, 0, UNITS), (3, second_products, 0, UNITS)]
            routing = shared[:1] + [(0, routing_products, 0, UNITS)] + shared[1:]
            both = shared[:1] + [(0, turn_hot, ROUND * ATT, UNITS), (1, pick, ROUND * ATT, UNITS)] + shared[1:]
            straight(0, 2 * ROUND, routing)
            rounds(pe, 2, ATT, shared)
            pe.wait_ge(table_ready, 1)
            straight(ROUND * ATT, ROUND * (ATT + 1), both)
            rounds(pe, ATT + 1, UNITS // ROUND, both)
            straight(UNITS, UNITS + 3, both)

            pe.wait_ge(y_read, NB)
            pe.wait_ge(v_read, APAIRS)

            pairs = []

            def load_pairs(g):
                n = 2 * RING if past(g, 1) else RING
                _, values = nc.values_load_multi_w_load_instructions(
                    experts[0:1, bass.ds(RING * g + RING - n, n), :].rearrange("p t k -> p (t k)"),
                    engines=(mybir.EngineType.PE,), min_val=NSH, max_val=NE - 1,
                    skip_runtime_bounds_check_because="the table's entries are NSH plus sums of steps between experts")
                pairs[:] = [None] * (2 * RING - n) + [values[2 * i:2 * i + 2] for i in range(n)]

            def r_turn(g, r):
                t = RING * g + r
                pe.wait_ge(d_in[r], 16 * (g + 1))
                for s in range(2):
                    mm = pe.transpose(pT16[:, s * P:(s + 1) * P], xr16[:, r, s * P:(s + 1) * P], c["ident"][:])
                mm.then_inc(d_turn, 1)

            def r_first(g, r):
                t = RING * g + r
                pe.wait_ge(d_xt, t + 1)
                for k, e in enumerate(pairs[RING - 1 if r == RING - 1 else RING + r]):
                    o = pAB[:, 2 * (r % 2) + k, :]
                    hi, lo = (wsp[:, s, bass.ds(e, 1), 0:2 * HID].rearrange("p o c -> p (o c)") for s in range(2))
                    pe.matmul(o, xrT[:, r, 0:P], hi, start=True, stop=False)
                    pe.matmul(o, xrT[:, r, P:2 * P], hi, start=False, stop=False)
                    mm = pe.matmul(o, xrT[:, r, 0:P], lo, start=False, stop=True)
                mm.then_inc(d_l1, 1)

            def r_hturn(g, r):
                t = RING * g + r
                pe.wait_ge(d_lo, t + 1)
                for s, part in enumerate((h_hi, h_lo)):
                    for k in range(4):
                        mm = pe.transpose(pY16[:, s, k * P:(k + 1) * P],
                                          part[:, r % 2, k * P:(k + 1) * P], c["ident"][:])
                mm.then_inc(d_hturn, 1)

            def r_second(g, r):
                t = RING * g + r
                pe.wait_ge(d_hT_hi, t + 1)
                pe.wait_ge(d_hT_lo, t + 1)
                for k, e in enumerate(pairs[r]):
                    for h in range(2):
                        w = slice(W2 + h * P, W2 + (h + 1) * P)
                        q = 2 * k + h
                        both = wsp[:, :, bass.ds(e, 1), w].rearrange("p s o c -> p s (o c)")
                        hi = wsp[:, 0, bass.ds(e, 1), w].rearrange("p o c -> p (o c)")
                        pe.matmul(pS.rearrange("p (s c) -> p s c", s=2),
                                  h_hi[:, 2 + r % 2, q * P:(q + 1) * P], both,
                                  start=(q == 0), stop=False, skip_group_check=True)
                        mm = pe.matmul(pS[:, 0:P], h_lo[:, 2 + r % 2, q * P:(q + 1) * P], hi,
                                       start=False, stop=(q == 3), skip_group_check=True)
                mm.then_inc(d_l2, 1)

            pipeline(pe, ROUTED, RING, 2, [(4, r_second), (3, r_hturn), (1, r_first), (0, r_turn)], begin=load_pairs)

        @block.scalar
        def _(act):
            for dst, src in [(wp_raw[:], wproj), (bp[:], bproj), (wo[:], w_out), (bo_raw[:], b_out)] + [
                    (c[k] if k == "pair_ids" else c[k][:], const[k]) for k in const]:
                act.dma_start(dst, src).then_inc(const_in, 16)
            for r in range(2):
                act.dma_start(wraw[:, r, :], wall[r]).then_inc(w_in[r], 16)
            act.wait_ge(const_in, 16 * n_const)
            nc.scalar.activation(wp[:, 0, :], wp_raw[:], ACT.Copy, scale=WS).then_inc(wp_hi, 1)
            act.wait_ge(bo_zero, 1)

            def split_high(g, r):
                act.wait_ge(w_in[r], 16 * (g + 1))
                nc.scalar.activation(whi[:, bass.ds(2 * g + r, 1), :].rearrange("p o c -> p (o c)"),
                                     wraw[:, r, :], ACT.Copy, scale=WS).then_inc(w_split_hi, 1)

            nc.scalar.activation(bo[0:1, 0, :], bo_raw[:], ACT.Copy, scale=WS).then_inc(wp_hi, 1)
            act.wait_ge(var_ready, 1)
            nc.scalar.activation(st[:, 5, :], st[:, 4, :], ACT.Sqrt).then_inc(root_ready, 1)

            def rows_high(g, r):
                i = 4 * g + r
                act.wait_ge(xs_ready, i + 1)
                nc.scalar.copy(rows16[:, bass.ds(TPB * i, TPB), 0:P], xs[:, r, :, :]).then_inc(rows_hi, 1)

            def turned_copy(g, r):
                i = 4 * g + r
                act.wait_ge(turned, i + 1)
                for s, bank in enumerate((pA, pB)):
                    a = nc.scalar.copy(xT[:, bass.ds(i, 1), s, :].rearrange("p o c -> p (o c)"), bank[:, r % 2, :])
                a.then_inc(xt_ready, 1)

            
            def shared_high(g, r):
                if g == 1 and r < NSH:
                    split_high(0, r)

            pipeline(act, NB, 4, 4, [(0, rows_high), (0, shared_high), (2, turned_copy)])

            def exponentials(g, u):
                n = ROUND * g + u
                if n == GAP_UNIT:
                    act.wait_ge(gap_ready, 1)
                    nc.scalar.activation(rt[:, 5, :], rt[:, 4, :], ACT.Exp).then_inc(gap_exp, 1)
                if n == LOGIT_UNIT:
                    act.wait_ge(logit_ready, 1)
                    nc.scalar.activation(weight, weight, ACT.Exp).then_inc(logit_exp, 1)

            def silu_unit(b, u):
                n = 8 * b + u
                act.wait_ge(l1, n + 1)
                if past(n, 2):
                    act.wait_ge(hf_done, n - 1)
                nc.scalar.activation(silu[:, u % 2, :], pA[:, u % 2, :], ACT.Silu,
                                     scale=1 / (XS * WS)).then_inc(silu_done, 1)

            def hi_unit(b, u):
                n = 8 * b + u
                act.wait_ge(hf_done, n + 1)
                if past(n, 4):
                    act.wait_ge(l2, n - 3)
                nc.scalar.copy(h_hi[:, u % 4, :], hf[:, u % 2, :]).then_inc(hi_done, 1)

            def hot_copy(g, u):
                m = ROUND * (g - ATT) + u
                act.wait_ge(hot_turned, m + 1)
                if past(m, 2):
                    act.wait_ge(v_done, m - 1)
                nc.scalar.copy(hotT[:, u % 2, :], pV16[:, 0, :]).then_inc(hotT_ready, 1)

            def routed_high(g, u):
                if u % 4 == 1:
                    split_high(g - (ATT - 1), u // 4)

            shared = [(0, silu_unit, 0, UNITS), (1, hi_unit, 0, UNITS)]
            routing = shared[:1] + [(0, exponentials, 0, UNITS)] + shared[1:]
            both = shared[:1] + [(0, hot_copy, ROUND * ATT, UNITS)] + shared[1:] + [(0, routed_high, ROUND * ATT, UNITS)]
            straight(0, 2 * ROUND, routing)
            rounds(act, 2, ATT, shared)
            act.wait_ge(scratch_free, 1)
            straight(ROUND * ATT, ROUND * (ATT + 1), both)
            rounds(act, ATT + 1, UNITS // ROUND, both)
            straight(UNITS, UNITS + 3, both)

            act.wait_ge(hf_done, 4 * NB)
            act.wait_ge(l2, 4 * NB)

            def r_xt(g, r):
                t = RING * g + r
                act.wait_ge(d_turn, t + 1)
                nc.scalar.copy(xrT[:, r, :], pT16).then_inc(d_xt, 1)

            def r_silu(g, r):
                t = RING * g + r
                act.wait_ge(d_l1, t + 1)
                nc.scalar.activation(silu[:, r % 2, :].rearrange("p (k c) -> p k c", k=2),
                                     pAB[:, 2 * (r % 2):2 * (r % 2) + 2, 0:HID], ACT.Silu,
                                     scale=1 / (XS * WS)).then_inc(d_silu, 1)

            def r_hi(g, r):
                t = RING * g + r
                act.wait_ge(d_hf, t + 1)
                nc.scalar.copy(h_hi[:, r % 2, :], hf[:, r % 2, :]).then_inc(d_hi, 1)

            def r_hT_hi(g, r):
                t = RING * g + r
                act.wait_ge(d_hturn, t + 1)
                nc.scalar.copy(h_hi[:, 2 + r % 2, :], pY16[:, 0, 0:512]).then_inc(d_hT_hi, 1)

            pipeline(act, ROUTED, RING, 2, [(2, r_silu), (1, r_xt), (2, r_hi), (3, r_hT_hi)])

            with act.Fori(0, NB) as i:
                act.wait_ge(fin, i + 1)
                act.dma_start(out_blk[bass.ds(i, 1)].rearrange("o p w -> p (o w)"),
                              base_blk[:, bass.ds(i, 1), :].rearrange("p o w -> p (o w)")).then_inc(out_done, 16)
            act.wait_ge(out_done, 16 * NB)

        @block.gpsimd
        def _(pool):
            nc.gpsimd.memset(bo[:], 0.0).then_inc(bo_zero, 1)
            nc.gpsimd.memset(rows[:, :, 2 * P // 2:ROWW], 0).then_inc(meta_init, 1)
            pool.wait_ge(const_in, 16 * n_const)
            pool.wait_ge(meta_init, 1)
            nc.gpsimd.tensor_copy(rows[:, :, TOKW:TOKW + 1], c["token"][:].unsqueeze(2)).then_inc(meta_init, 1)

            def rows_low(g, r):
                i = 4 * g + r
                pool.wait_ge(rows_hi, i + 1)
                pool.sem_inc(pool_go, 1)
                nc.gpsimd.tensor_tensor(rows16[:, bass.ds(TPB * i, TPB), P:2 * P], xs[:, r, :, :],
                                        rows16[:, bass.ds(TPB * i, TPB), 0:P], ALU.subtract).then_inc(rows_lo, 1)

            pipeline(pool, NB, 4, 1, [(0, rows_low)])

            rows_due = lambda n: max(0, n + 1 - SCATTER_UNIT) * NT // (UNITS - SCATTER_UNIT)
            for n in range(UNITS):
                if n == SCATTER_UNIT:
                    pool.wait_ge(slot_ready, 1)
                    pool.wait_ge(cw_ready, 1)
                    pool.wait_ge(pad_out, 16)
                for t in range(rows_due(n - 1), rows_due(n)):
                    pool.indirect_dma_start(sorted_rows,
                                            bass.IndirectOffsetOnAxis(ap=slot[:, t:t + 1].bitcast(U32), axis=0),
                                            rows[:, t, :], None, bounds_check=SLOTS - 1).then_inc(sorted_in, 16)
                pool.wait_ge(hi_done, n + 1)
                nc.gpsimd.tensor_tensor(h_lo[:, n % 4, :], hf[:, n % 2, :], h_hi[:, n % 4, :],
                                        ALU.subtract).then_inc(lo_done, 1)

            def r_lo(g, r):
                t = RING * g + r
                pool.wait_ge(d_hi, t + 1)
                pool.sem_inc(pool_go, 1)
                nc.gpsimd.tensor_tensor(h_lo[:, r % 2, :], hf[:, r % 2, :], h_hi[:, r % 2, :],
                                        ALU.subtract).then_inc(d_lo, 1)

            def r_scatter(g, r):
                pool.wait_ge(d_y, RING * g + r + 1)
                pool.sem_inc(pool_go, 1)
                pool.indirect_dma_start(y_rows, bass.IndirectOffsetOnAxis(ap=yidx[:, r:r + 1].bitcast(U32), axis=0),
                                        yt[:, r, :], None, bounds_check=TOK - 1, oob_is_err=False).then_inc(d_out[r], 16)

            pipeline(pool, ROUTED, RING, 2, [(2, r_lo), (4, r_scatter)])

        @block.vector
        def _(dve):
            v = nc.vector
            steps = [0]

            def then(ins):
                steps[0] += 1
                ins.then_inc(dv, 1)
                dve.wait_ge(dv, steps[0])

            def split_low(g, r):
                row = lambda a: a[:, bass.ds(2 * g + r, 1), :].rearrange("p o c -> p (o c)")
                dve.wait_ge(w_split_hi, 2 * g + r + 1)
                v.scalar_tensor_tensor(row(wlo), wraw[:, r, :], WS, row(whi), ALU.mult, ALU.subtract).then_inc(w_split, 1)

            for q in range(NQ):
                dve.wait_ge(x_in[q], 16)
                for t in range(NT // NQ * q, NT // NQ * (q + 1)):
                    ins = v.bn_stats(stats[:, t, :], base[:, t, :])
                ins.then_inc(stats_done, 1)
            dve.wait_ge(stats_done, NQ)
            half = lambda k: stats[:, :, k]
            v.tensor_tensor(st[:, 0, :], half(1), half(4), ALU.add)
            v.tensor_tensor(st[:, 2, :], half(2), half(5), ALU.add)
            then(v.tensor_tensor(st[:, 1, :], half(1), half(4), ALU.subtract))
            then(v.scalar_tensor_tensor(st[:, 3, :], st[:, 1, :], P / 4.0, st[:, 1, :], ALU.mult, ALU.mult))
            then(v.tensor_tensor(st[:, 2, :], st[:, 2, :], st[:, 3, :], ALU.add))
            v.tensor_scalar(st[:, 4, :], st[:, 2, :], 1.0 / P, EPS, ALU.mult, ALU.add).then_inc(var_ready, 1)
            then(v.tensor_scalar(st[:, 0, :], st[:, 0, :], 0.5, None, ALU.mult))
            dve.wait_ge(csum_done, 1)
            then(v.tensor_scalar(csum[:], pY[:, 1, 0:P], 1 / XS, None, ALU.mult))
            dve.wait_ge(wp_hi, 1)
            v.scalar_tensor_tensor(wp[:, 1, :], wp_raw[:], WS, wp[:, 0, :], ALU.mult, ALU.subtract).then_inc(small_split, 1)
            dve.wait_ge(wp_hi, 2)
            v.scalar_tensor_tensor(bo[0:1, 1, :], bo_raw[:], WS, bo[0:1, 0, :], ALU.mult, ALU.subtract).then_inc(small_split, 1)

            dve.wait_ge(root_ready, 1)
            then(v.reciprocal(st[:, 6, :], st[:, 5, :]))
            then(v.tensor_tensor(st[:, 6, :], st[:, 6, :], st[:, 4, :], ALU.mult))
            then(v.tensor_tensor(st[:, 6, :], st[:, 6, :], st[:, 5, :], ALU.add))
            then(v.reciprocal(st[:, 7, :], st[:, 6, :]))
            then(v.tensor_scalar(st[:, 7, :], st[:, 7, :], 2 * XS, None, ALU.mult))

            def normalise(g, r):
                i = 4 * g + r
                if past(i, 4):
                    dve.wait_ge(rows_lo, i - 3)
                for j in range(TPB):
                    t = TPB * i + j
                    ins = v.tensor_scalar(xs[:, r, j, :], base[:, bass.ds(t, 1), :].rearrange("p o c -> p (o c)"),
                                          st[:, 0, bass.ds(t, 1)], st[:, 7, bass.ds(t, 1)], ALU.subtract, ALU.mult)
                ins.then_inc(xs_ready, 1)

            def read_projections(g, r):
                i = 4 * g + r
                dve.wait_ge(proj_done, i + 1)
                v.scalar_tensor_tensor(proj[:, bass.ds(TPB * i, TPB), :],
                                       pV[:, r % 2, 0:TPB * PROJ].rearrange("p (j c) -> p j c", c=PROJ), 1 / (XS * WS),
                                       bp[:].unsqueeze(1).broadcast_to([P, TPB, PROJ]),
                                       ALU.mult, ALU.add).then_inc(proj_read, 1)

            def shared_low(g, r):
                if g == 1 and r >= 4 - NSH:
                    split_low(0, r - (4 - NSH))

            pipeline(dve, NB, 4, 4, [(0, normalise), (0, shared_low), (3, read_projections)])

            def hf_unit(b, u):
                n = 8 * b + u
                dve.wait_ge(silu_done, n + 1)
                if past(n, 2):
                    dve.wait_ge(lo_done, n - 1)
                v.scalar_tensor_tensor(hf[:, u % 2, :], pB[:, u % 2, :], 1 / (XS * WS), silu[:, u % 2, :],
                                       ALU.mult, ALU.mult).then_inc(hf_done, 1)

            def add_shared(b, u):
                if u % 4 != 3:
                    return
                i = 2 * b + u // 4
                dve.wait_ge(l2, 4 * i + 4)
                row = base_blk[:, bass.ds(i, 1), :].rearrange("p o w -> p (o w)")
                v.scalar_tensor_tensor(row, pY[:, u // 4, :], 1 / WS, row, ALU.mult, ALU.add).then_inc(y_read, 1)

            shared_parts = [(0, hf_unit, 0, UNITS), (4, add_shared, 0, UNITS)]
            unit = [0]

            def shared_unit():
                straight(unit[0], unit[0] + 1, shared_parts)
                unit[0] += 1

            dve.wait_ge(proj_read, NB)

            logits = proj[:, :, 2 * HP:PROJ]
            wide8 = lambda a: a.unsqueeze(2).broadcast_to([P, NT, E])
            from_last = c["from_last"][:].unsqueeze(1).broadcast_to([P, NT, E])

            def largest(values, eq, score, out_max, out_rank):
                then(v.tensor_reduce(out_max, values, AX.X, ALU.max))
                then(v.tensor_tensor(eq, values, wide8(out_max), ALU.is_equal))
                then(v.tensor_tensor(score, eq, from_last, ALU.mult))
                then(v.tensor_reduce(out_rank, score, AX.X, ALU.max))

            largest(logits, r8[:, 0], r8[:, 1], rt[:, 0, :], rt[:, 1, :])
            shared_unit()
            then(v.tensor_tensor(r8[:, 2], r8[:, 1], wide8(rt[:, 1, :]), ALU.is_equal))
            then(v.scalar_tensor_tensor(r8[:, 3], r8[:, 2], -1e30, logits, ALU.mult, ALU.add))
            shared_unit()
            largest(r8[:, 3], r8[:, 0], r8[:, 1], rt[:, 2, :], rt[:, 3, :])
            v.tensor_tensor(rt[:, 4, :], rt[:, 2, :], rt[:, 0, :], ALU.subtract).then_inc(gap_ready, 1)
            shared_unit()
            then(v.tensor_tensor(rt[:, 6, :], rt[:, 1, :], rt[:, 3, :], ALU.max))
            then(v.tensor_tensor(rt[:, 7, :], rt[:, 1, :], rt[:, 3, :], ALU.min))
            then(v.tensor_scalar(rt[:, 8, :], rt[:, 6, :], -1.0, float(E), ALU.mult, ALU.add))
            then(v.tensor_scalar(rt[:, 9, :], rt[:, 6, :], 0.5, 2.5, ALU.mult, ALU.add))
            then(v.tensor_tensor(rt[:, 8, :], rt[:, 8, :], rt[:, 9, :], ALU.mult))
            then(v.tensor_tensor(rt[:, 8, :], rt[:, 8, :], rt[:, 7, :], ALU.subtract))
            then(v.tensor_scalar(pair16[:], rt[:, 8, :], E - 1.0, None, ALU.add))
            shared_unit()

            scan, place = scratch_a[:, 0:NPAIR * NT], scratch_b[:, 0:NPAIR * NT]
            scan3, place3 = (a.rearrange("p (q t) -> p q t", q=NPAIR) for a in (scan, place))
            then(v.tensor_tensor(member, pair16[:].unsqueeze(1).broadcast_to([P, NPAIR, NT]),
                                 c["pair_ids"].rearrange("p (q t) -> p q t", q=NPAIR), ALU.is_equal))
            shared_unit()
            then(v.tensor_tensor_scan(scan, member_row, member_row, 0.0, ALU.add, ALU.max))
            then(v.memset(seg[:, 0, :], 0.0))
            then(v.tensor_copy(seg[:, 0, 1:NPAIR], scan3[:, 0:NPAIR - 1, NT - 1]))
            v.tensor_tensor(seg16[:], scan3[:, :, NT - 1], seg[:, 0, :], ALU.subtract).then_inc(seg_ready, 1)
            shared_unit()
            dve.wait_ge(gap_exp, 1)
            then(v.tensor_scalar(rt[:, 6, :], rt[:, 5, :], 1.0, None, ALU.add))
            then(v.reciprocal(rt[:, 7, :], rt[:, 6, :]))
            then(v.tensor_scalar(rt[:, 7, :], rt[:, 7, :], 1 / (XS * WS), None, ALU.mult))
            then(v.tensor_tensor(rt[:, 8, :], rt[:, 7, :], rt[:, 5, :], ALU.mult))
            then(v.tensor_tensor(rt[:, 9, :], rt[:, 7, :], rt[:, 8, :], ALU.subtract))
            then(v.tensor_tensor(rt[:, 10, :], rt[:, 1, :], rt[:, 3, :], ALU.is_gt))
            then(v.tensor_tensor(rt[:, 9, :], rt[:, 9, :], rt[:, 10, :], ALU.mult))
            dve.wait_ge(meta_init, 2)
            then(v.tensor_tensor(rows32[:, :, CWA], rt[:, 8, :], rt[:, 9, :], ALU.add))
            v.tensor_tensor(rows32[:, :, CWB], rt[:, 7, :], rt[:, 9, :], ALU.subtract).then_inc(cw_ready, 1)
            shared_unit()
            assert unit[0] >= SEG_UNIT
            dve.wait_ge(seg_done, 1)
            then(v.tensor_scalar(segi[:, 0, :], pV[:, 0, 32:32 + NPAIR], P - 1.0, None, ALU.add))
            then(v.tensor_scalar(segi[:, 1, :], segi[:, 0, :], 7, None, ALU.logical_shift_right))
            then(v.tensor_copy(seg[:, 1, :], segi[:, 1, :]))
            then(v.tensor_tensor_scan(seg[:, 2, :], seg[:, 1, :], seg[:, 1, :], 0.0, ALU.add, ALU.max))
            then(v.tensor_tensor(seg[:, 3, :], seg[:, 2, :], seg[:, 1, :], ALU.subtract))
            then(v.scalar_tensor_tensor(seg[:, 4, :], seg[:, 3, :], float(P), pV[:, 0, 0:NPAIR], ALU.mult, ALU.add))
            then(v.scalar_tensor_tensor(seg[:, 5, :], seg[:, 4, :], -1.0, seg[:, 0, :], ALU.add, ALU.subtract))
            then(v.tensor_tensor(place3, scan3, seg[:, 5, :].unsqueeze(2).broadcast_to([P, NPAIR, NT]), ALU.add))
            shared_unit()
            then(v.tensor_tensor(place, place, member_row, ALU.mult))
            shared_unit()
            then(v.tensor_reduce(rt[:, 11, :], place3.rearrange("p q t -> p t q"), AX.X, ALU.add))
            v.tensor_copy(slot[:], rt[:, 11, :]).then_inc(slot_ready, 1)
            shared_unit()

            then(v.tensor_scalar(tab_scr[:, 0, :], seg[:, 3, :], c["part"][:], None, ALU.is_le))
            for k, name in enumerate(("pair_step_a", "pair_step_b")):
                then(v.tensor_tensor_reduce(tab_scr[:, 1, :], tab_scr[:, 0, :], c[name][:], 1.0, 0.0,
                                            ALU.mult, ALU.add, tab_f[:, k:k + 1]))
            v.tensor_copy(tab16[:], tab_f[:]).then_inc(tab_ready, 1)
            first_row = xT[:, 0:NB:2, :, 0].unsqueeze(3).broadcast_to([P, BATCH, 2, HI16 * GRP])
            mask = c["high_mask"][:].unsqueeze(1).unsqueeze(1).broadcast_to([P, BATCH, 2, HI16 * GRP])
            dve.wait_ge(xt_ready, NB)
            then(v.tensor_tensor(tsel.rearrange("p (b s) c -> p b s c", s=2), mask, first_row, ALU.mult))
            shared_unit()

            weight4 = weight.rearrange("p t (h k) -> p t h k", k=POINTS)
            wide4 = lambda a: a.unsqueeze(3).broadcast_to([P, NT, HEADS, POINTS])
            then(v.tensor_reduce(wmax[:, 0], weight4, AX.X, ALU.max))
            shared_unit()
            assert unit[0] >= TAB_UNIT
            dve.wait_ge(tab_done, 1)
            then(v.tensor_scalar(experts[:].rearrange("p t k -> p k t"),
                                 pV[0:1, 0, P:3 * P].rearrange("p (k t) -> p k t", k=2), float(NSH), None, ALU.add))
            v.memset(seg[:, 0, 1:2], 0.0).then_inc(tsel_ready, 1)
            v.tensor_tensor(weight4, weight4, wide4(wmax[:, 0]), ALU.subtract).then_inc(logit_ready, 1)
            shared_unit()

            size = scratch_b.rearrange("p (t k) -> p t k", k=HP)
            whole = scratch_a.bitcast(I32).rearrange("p (t k) -> p t k", k=HP)
            fl = [a.rearrange("p (t k) -> p t k", k=HP) for a in fl16]
            idx3 = idx.rearrange("p (t k) -> p t k", k=HP)
            then(v.tensor_scalar(offsets, offsets, 127.5, -128.0, ALU.min, ALU.max))
            shared_unit()
            assert unit[0] >= TABLE_UNIT
            dve.wait_ge(table_done, 1)
            same = c["same_gather"][:].unsqueeze(1).broadcast_to([P, 8, HI16 * GRP])
            for k in range(2):
                ins = v.tensor_tensor(table[:, 4 * k:4 * k + 4].rearrange("p b s c -> p (b s) c"),
                                      pV[:, k, :].rearrange("p (g c) -> p g c", g=8), same, ALU.mult)
            ins.then_inc(table_ready, 1)
            shared_unit()
            then(v.scalar_tensor_tensor(size, offsets, -1.0, offsets, ALU.mult, ALU.max))
            shared_unit()
            then(v.tensor_copy(whole, size))
            shared_unit()
            then(v.scalar_tensor_tensor(fl[0], whole, 0.0, size, ALU.add, ALU.is_gt))
            shared_unit()
            then(v.tensor_tensor(fl[1], whole, fl[0], ALU.subtract))
            shared_unit()
            then(v.tensor_scalar(fl[0], fl[1], -2.0, float(P), ALU.mult, ALU.add))
            then(v.scalar_tensor_tensor(fl[0], offsets, 0.0, fl[0], ALU.is_lt, ALU.mult))
            shared_unit()
            then(v.tensor_tensor(idx3, fl[1], fl[0], ALU.add))
            shared_unit()
            then(v.tensor_scalar(ilo, idx3, LO16 - 1, None, ALU.bitwise_and))
            then(v.tensor_scalar(ihi, idx3, 4, HI16 - 1, ALU.logical_shift_right, ALU.bitwise_and))
            shared_unit()

            assert unit[0] >= LOGIT_UNIT
            dve.wait_ge(logit_exp, 1)
            then(v.tensor_reduce(wmax[:, 1], weight4, AX.X, ALU.add))
            shared_unit()
            then(v.reciprocal(wmax[:, 0], wmax[:, 1]))
            shared_unit()
            then(v.tensor_tensor(weight4, weight4, wide4(wmax[:, 0]), ALU.mult))
            v.memset(seg[:, 0, 0:1], 0.0).then_inc(scratch_free, 1)
            shared_unit()

            def one_hot(g, u):
                half = (ROUND // 2) * (g - ATT) + (u // 2 + 1)
                if u % 2 == 0 and past(half, 2):
                    dve.wait_ge(hot_turned, 2 * half - 2)
                src = proj_i16[:, bass.ds(TPB * half, TPB), 0:HP].rearrange("p t (g h) -> p t g h", h=GRP)
                for k in range(LO16 // 2 * (u % 2), LO16 // 2 * (u % 2 + 1)):
                    ins = v.tensor_scalar(hot[:, (u // 2 + 1) % 2, :, :, k, :], src, float(k), None, ALU.is_equal)
                if u % 2 == 1:
                    ins.then_inc(hot_ready, 1)

            def weighted_high(g, u):
                half = (ROUND // 2) * (g - ATT) + (u // 2 + 1)
                if u % 2 == 0 and past(half, 2):
                    dve.wait_ge(v_read, 2 * half - 2)
                tiles = bass.ds(TPB * half, TPB)
                src = proj_i16[:, tiles, HP:2 * HP].rearrange("p t (g h) -> p t g h", h=GRP)
                w = proj[:, tiles, HP:2 * HP].rearrange("p t (g h) -> p t g h", h=GRP)
                for k in range(HI16 // 2 * (u % 2), HI16 // 2 * (u % 2 + 1)):
                    ins = v.scalar_tensor_tensor(aw[:, (u // 2 + 1) % 2, :, :, k, :], src, float(k), w,
                                                 ALU.is_equal, ALU.mult)
                if u % 2 == 1:
                    ins.then_inc(aw_ready, 1)

            def weigh(g, u):
                m = ROUND * (g - ATT) + u
                if u % 4 == 0 and past(m, 8):
                    dve.wait_ge(attn_saved, 2 * (g - ATT) + (u // 4 - 1))
                if u % 2 == 0:
                    dve.wait_ge(aw_ready, (ROUND // 2) * (g - ATT) + (u // 2 + 1))
                dve.wait_ge(v_done, m + 1)
                for t in range(2):
                    ins = v.tensor_tensor_reduce(vscr[:, t, :], pV[:, 1, t * 256:(t + 1) * 256],
                                                 aw[:, (u // 2) % 2, 2 * (u % 2) + t].rearrange("p g a h -> p (g a h)"),
                                                 1.0, 0.0, ALU.mult, ALU.add,
                                                 attn[:, u // 4, 2 * (u % 4) + t:2 * (u % 4) + t + 1])
                ins.then_inc(v_read, 1)

            def keep_sums(g, u):
                if u % 4 == 3:
                    m = ROUND * (g - ATT) + u
                    dve.wait_ge(v_read, m + 1)
                    v.tensor_copy(attn_all[:, bass.ds(ROUND * (2 * (g - ATT) + u // 4), 8)],
                                  attn[:, u // 4, :]).then_inc(attn_saved, 1)

            def routed_low(g, u):
                if u % 4 == 2:
                    split_low(g - (ATT - 1), u // 4)

            while unit[0] < ROUND * ATT - 2:
                shared_unit()
            for u in (ROUND - 2, ROUND - 1):
                shared_unit()
                one_hot(ATT - 1, u)
                weighted_high(ATT - 1, u)

            start, end = ROUND * ATT, UNITS
            both = shared_parts[:1] + [(0, one_hot, start, end - 2), (1, weigh, start, end),
                                       (0, weighted_high, start, end - 2), (1, keep_sums, start, end),
                                       (0, routed_low, start, end)] + shared_parts[1:]
            straight(start, start + ROUND, both)
            rounds(dve, ATT + 1, UNITS // ROUND - 1, both)
            straight(UNITS - ROUND, UNITS + 4, both)

            dve.wait_ge(lo_done, 4 * NB)

            def r_meta(g, r):
                dve.wait_ge(d_in[r], 16 * (g + 1))
                if past(RING * g + r, RING):
                    dve.wait_ge(d_y, RING * g + r - RING + 1)
                v.tensor_copy(meta[:, r, :], xr[:, r, CWA:CWA + 4]).then_inc(d_meta, 1)

            def r_hf(g, r):
                t = RING * g + r
                dve.wait_ge(d_meta, t + 1)
                dve.wait_ge(d_silu, t + 1)
                for k in range(2):
                    ins = v.scalar_tensor_tensor(hf[:, r % 2, k * HID:(k + 1) * HID],
                                                 pAB[:, 2 * (r % 2) + k, HID:2 * HID], meta32[:, r, k:k + 1],
                                                 silu[:, r % 2, k * HID:(k + 1) * HID], ALU.mult, ALU.mult)
                ins.then_inc(d_hf, 1)

            def r_hT_lo(g, r):
                t = RING * g + r
                dve.wait_ge(d_hturn, t + 1)
                v.tensor_copy(h_lo[:, 2 + r % 2, :], pY16[:, 1, 0:512]).then_inc(d_hT_lo, 1)

            def r_y(g, r):
                t = RING * g + r
                dve.wait_ge(d_l2, t + 1)
                if past(t, RING):
                    dve.wait_ge(d_out[r], 16 * g)
                v.tensor_reduce(yt[:, r, :], pS.rearrange("p (s c) -> p c s", s=2), AX.X, ALU.add)
                v.tensor_copy(yidx[:, r:r + 1], meta[:, r, 2:3]).then_inc(d_y, 1)

            def add_attention(tile):
                row = base[:, bass.ds(tile, 1), :].rearrange("p o c -> p (o c)")
                return v.scalar_tensor_tensor(row, csum[:], attn_all[:, bass.ds(tile, 1)], row, ALU.mult, ALU.add)

            peel = 2
            for_each = ROUTED // RING - peel
            adds = NT // for_each

            def r_attention(g, r):
                if not isinstance(g, int) and r < adds:
                    add_attention(adds * (g - peel) + r)

            dve.wait_ge(y_read, NB)
            dve.wait_ge(attn_saved, BATCH)
            pipeline(dve, ROUTED, RING, peel, [(2, r_hf), (4, r_y), (3, r_hT_lo), (0, r_meta), (0, r_attention)])
            for tile in range(adds * for_each, NT):
                ins = add_attention(tile)
            ins.then_inc(attn_added, 1)

            dve.wait_ge(attn_added, 1)
            dve.wait_ge(y_read, NB)
            with dve.Fori(0, NB // 4) as q:
                for r in range(4):
                    dve.wait_ge(y_in[r], 16 * (q + 1))
                    tiles = base[:, bass.ds(4 * (4 * q + r), TPB), :]
                    v.scalar_tensor_tensor(tiles, y_all[:, bass.ds(4 * (4 * q + r), TPB), :], 1 / WS, tiles,
                                           ALU.mult, ALU.add).then_inc(fin, 1)


def kernel(**inputs):
    import concourse.bacc as _bacc
    from concourse.bass_utils import run_bass_kernel_spmd as _run

    a = {k.replace("L0_attn_", "").replace("L0_ffn_", "f_"): np.asarray(v) for k, v in inputs.items()}
    wproj = np.concatenate([a["W_off"][:, 0::2], a["W_attn"], a["f_router_w"].T], axis=1)
    bproj = np.concatenate([a["b_off"][0::2], a["b_attn"], a["f_expert_bias"]])
    w1 = np.concatenate([a["f_sw1"], a["f_w1"]])
    w3 = np.concatenate([a["f_sw3"], a["f_w3"]])
    w2 = np.concatenate([a["f_sw2"], a["f_w2"]])
    by_half = w2.transpose(0, 2, 1).reshape(NE, HID // P, P, P).transpose(0, 2, 1, 3).reshape(NE, P, HID)
    wall = np.concatenate([w1.transpose(0, 2, 1), w3.transpose(0, 2, 1), by_half], axis=2)
    const = constants()
    arrays = {
        "x": a["x"], "wall": wall, "wproj": wproj, "bproj": np.broadcast_to(bproj[None, :], (P, PROJ)),
        "w_out": a["W_out"], "b_out": a["b_out"][None, :],
    }
    arrays = {k: np.ascontiguousarray(v) for k, v in arrays.items()}
    arrays |= {"c_" + k: np.ascontiguousarray(v) for k, v in const.items()}

    nc = _bacc.Bacc("TRN2", target_bir_lowering=False, num_devices=1)
    dram = {k: nc.dram_tensor("in_" + k, v.shape, mybir.dt.from_np(v.dtype), kind="ExternalInput").ap()
            for k, v in arrays.items()}
    out = nc.dram_tensor("out_dram", a["x"].shape, F32, kind="ExternalOutput").ap()
    sorted_rows = nc.dram_tensor("sorted_rows", [SLOTS, ROWW], I32, kind="Internal").ap()
    y_rows = nc.dram_tensor("y_rows", [TOK, P], F32, kind="Internal").ap()
    consts = {k: dram["c_" + k] for k in const}
    layer_kernel(nc, dram["x"], dram["wall"], dram["wproj"], dram["bproj"], dram["w_out"], dram["b_out"],
                 consts, out, sorted_rows, y_rows)
    got = _run(nc, [{"in_" + k: v for k, v in arrays.items()}], core_ids=[0])
    return got.results[0]["out_dram"]
```

```python
from contextlib import ExitStack

import numpy as np

import concourse.bass as bass
from concourse import mybir

ALU = mybir.AluOpType
ACT = mybir.ActivationFunctionType
AX = mybir.AxisListType
F32 = mybir.dt.float32
F16 = mybir.dt.float16
I32 = mybir.dt.int32
I16 = mybir.dt.int16
U32 = mybir.dt.uint32

P = 128
BATCH, SEQ = 8, 1024
TOK = BATCH * SEQ
NT = TOK // P
BLK = 512
TPB = BLK // P
NB = TOK // BLK
TPS = SEQ // P
HEADS, POINTS = 8, 4
HP = HEADS * POINTS
E, NSH, HID = 8, 2, 256
NE = E + NSH
CHOICES = 2
PROJ = 2 * HP + E
NQ = 4
RING = 4
STEPS = -(-((CHOICES * TOK + E * (P - 1)) // P) // (2 * RING)) * RING
SLOTS = STEPS * 2 * P
ROWW = 130
CW, DEST = 128, 129
XS = 4096.0
WS = 64.0
EPS = 1e-5
LO16, HI16 = 16, 8
GRP = 8
NG = HP // GRP
W1, W3, W2 = 0, HID, 2 * HID
WCOL = 3 * HID
UNITS = TOK // BLK * NSH * 2
ROUND = 8
ATT = 4
APAIRS = NT // 2
EARLY_ROWS = 3
LAST_LOW = UNITS - 3
GAP_UNIT, SEG_UNIT, TAB_UNIT, TABLE_UNIT, LOGIT_UNIT, SCATTER_UNIT = 3, 5, 9, 11, 11, 9


def constants():
    p = np.arange(P)
    b_of, h_of = p // GRP, p % GRP
    ah = np.arange(HI16 * GRP)
    a_of, g_of = ah // GRP, ah % GRP
    token = (np.arange(NT)[None, :] // TPB) * BLK + p[:, None] * TPB + np.arange(NT)[None, :] % TPB
    pad = np.zeros((P, ROWW), np.int32)
    pad[:, DEST] = CHOICES * TOK + p
    f16, f32 = np.float16, np.float32
    wide = lambda v: np.broadcast_to(v[None, :], (P, len(v)))
    return {
        "ident": np.eye(P, dtype=f16),
        "before": (p[:, None] < p[None, :]).astype(f16),
        "ones": np.ones((P, P), f16),
        "low_sel": (p[:, None] % LO16 == b_of[None, :]).astype(f16),
        "high_mask": (p[:, None] // LO16 == a_of[None, :]).astype(f16),
        "same_gather": (h_of[:, None] == g_of[None, :]).astype(f16),
        "from_last": wide(E - np.arange(E)).astype(f32),
        "tile": (p[:, None] + P * np.arange(2)[None, :]).astype(f32),
        "dest": np.stack([token, token + TOK], axis=1).astype(np.int32),
        "pad_row": pad,
        "ones32": np.ones((P, P), f32),
    }


def past(t, k):
    return not isinstance(t, int) or t >= k


def pipeline(eng, total, unroll, peel, parts, begin=lambda g: None):
    last = max(lag for lag, _ in parts)
    for s in range(unroll * peel):
        if s % unroll == 0:
            begin(s // unroll)
        for lag, part in parts:
            if s >= lag:
                part((s - lag) // unroll, (s - lag) % unroll)
    if peel < total // unroll:
        with eng.Fori(peel, total // unroll) as g:
            begin(g)
            for r in range(unroll):
                for lag, part in parts:
                    part(g + (r - lag) // unroll, (r - lag) % unroll)
    for s in range(total, total + last):
        if s % unroll == 0:
            begin(s // unroll)
        for lag, part in parts:
            if s - lag < total:
                part((s - lag) // unroll, (s - lag) % unroll)


def low_by_vector(n):
    return SCATTER_UNIT <= n < ROUND * ATT or n >= LAST_LOW


def straight(lo, hi, parts):
    for s in range(lo, hi):
        for lag, part, first, last in parts:
            if first <= s - lag < last:
                part((s - lag) // ROUND, (s - lag) % ROUND)


def rounds(eng, lo, hi, parts):
    with eng.Fori(lo, hi) as g:
        for u in range(ROUND):
            for lag, part, _, _ in parts:
                part(g + (u - lag) // ROUND, (u - lag) % ROUND)


def layer_kernel(nc, x, wall, wproj, bproj, w_out, b_out, const, out, sorted_rows, y_rows):
    with ExitStack() as ctx:
        def sb(name, shape, dt):
            return ctx.enter_context(nc.sbuf_tensor(name, shape, dt))

        def sem(name):
            return ctx.enter_context(nc.semaphore(name))

        pAB = ctx.enter_context(nc.psum_tensor("pAB", [P, 4, 512], F32))
        pA, pB = pAB[:, 0:2, :], pAB[:, 2:4, :]
        pY = ctx.enter_context(nc.psum_tensor("pY", [P, 2, 512], F32))
        pV = ctx.enter_context(nc.psum_tensor("pV", [P, 2, 512], F32))

        base = sb("base", [P, NT, P], F32)
        rows = sb("rows", [P, NT, ROWW], I32)
        xT = sb("xT", [P, NB, 2, BLK], F16)
        wsp = sb("wsp", [P, 2, NE, WCOL], F16)
        whi, wlo = wsp[:, 0], wsp[:, 1]
        wraw = sb("wraw", [P, 2, WCOL], F32)
        proj = sb("proj", [P, NT, PROJ], F32)
        wp_raw = sb("wp_raw", [P, PROJ], F32)
        wp = sb("wp", [P, 2, PROJ], F16)
        bp = sb("bp", [P, PROJ], F32)
        wo = sb("wo", [P, P], F32)
        csum = sb("csum", [P, P], F32)
        bo_raw = sb("bo_raw", [1, P], F32)
        bo = sb("bo", [P, 2, P], F16)
        units = sb("units", [P, 4, 512], F32)
        silu, hf = units[:, 0:2, :], units[:, 2:4, :]
        xs = units[:].rearrange("p r (j c) -> p r j c", j=TPB)
        h_hi = sb("h_hi", [P, 4, 512], F16)
        h_lo = sb("h_lo", [P, 4, 512], F16)
        c = {}
        hotT = sb("hotT", [P, 2, 8 * P], F16)
        for name, a in const.items():
            c[name] = sb("c_" + name, list(a.shape), a.dtype)
        hot = sb("hot", [P, 2, TPS, NG, LO16, GRP], F16)
        hot_row = hot[:].rearrange("p s t g b h -> p (s t g b h)")
        early = hot_row.bitcast(F32)
        stats = early[:, 0:6 * NT].rearrange("p (t k) -> p t k", k=6)
        st = early[:, 6 * NT:14 * NT].rearrange("p (k t) -> p k t", t=NT)
        rt = early[:, 14 * NT:26 * NT].rearrange("p (k t) -> p k t", t=NT)
        free_hi = whi[:, NSH:, :].rearrange("p e c -> p (e c)").bitcast(F32)
        free_lo = wlo[:, NSH:, :].rearrange("p e c -> p (e c)").bitcast(F32)
        r8 = free_hi[:, 0:6 * NT * E].rearrange("p (k t e) -> p k t e", k=6, t=NT)
        scratch_a = free_lo[:, 0:NT * HP]
        scratch_b = free_hi[:, 0:NT * HP]
        member = free_lo[:, NT * HP:].bitcast(F16)[:, 0:E * NT]
        scan, place = (scratch_a[:, k * E * NT:(k + 1) * E * NT].rearrange("p (e t) -> p e t", e=E) for k in range(2))
        seg = sb("seg", [P, 8, E], F32)
        seg16 = sb("seg16", [P, E], F16)
        segi = sb("segi", [P, 2, E], I32)
        cw = sb("cw", [P, CHOICES, NT], F32)
        slot = sb("slot", [P, CHOICES, NT], I32)
        tab16 = sb("tab16", [P, 2], F16)
        tab_scr = sb("tab_scr", [P, 2, E], F32)
        tab_f = sb("tab_f", [P, 2], F32)
        experts = sb("experts", [1, 2 * P], I32)
        aw = sb("aw", [P, 2, TPB, NG, HI16, GRP], F32)
        aw_row = aw[:].rearrange("p s t g b h -> p (s t g b h)")
        wmax = aw_row[:, 0:2 * NT * HEADS].rearrange("p (k t h) -> p k t h", k=2, h=HEADS)
        fl16 = [free_hi[:, NT * HP:].bitcast(F16), hot_row[:, 0:NT * HP]]
        idx = free_lo[:, NT * HP:].bitcast(I16)
        offsets = proj[:, :, 0:HP]
        weight = proj[:, :, HP:2 * HP]
        proj_i16 = proj[:].bitcast(I16)
        ilo, ihi = proj_i16[:, :, 0:HP], proj_i16[:, :, HP:2 * HP]
        table = sb("table", [P, BATCH, 2, HI16 * GRP], F16)
        attn = sb("attn", [P, 2, 8], F32)
        attn_all = sb("attn_all", [P, NT], F32)
        xr = (wraw[:].rearrange("p r c -> p (r c)")[:, 0:RING * 2 * ROWW].bitcast(I32)
              .rearrange("p (r k w) -> p r k w", r=RING, k=2))
        meta = sb("meta", [P, RING, 2, 2], I32)
        xrT = xT[:, 0:2].rearrange("p i s c -> p (i s c)").rearrange("p (r k s c) -> p r k s c", r=RING, k=2, s=2)
        yt = aw_row[:, 0:RING * 2 * P].rearrange("p (r k c) -> p r k c", r=RING, k=2)
        small = sb("small", [P, RING, P], F32)
        vscr = small[:].rearrange("p (t r) c -> p t (r c)", t=2)
        tsel = small[:].rearrange("p r c -> p (r c)").bitcast(F16).rearrange("p (g c) -> p g c", g=BATCH * 2)
        yidx = sb("yidx", [P, RING, 2], I32)

        y_all = [rows[:, :, 0:P].bitcast(F32),
                 xT[:].rearrange("p i s c -> p (i s c)").bitcast(F32).rearrange("p (t c) -> p t c", c=P)]
        rows16 = rows[:].bitcast(F16)
        rows32 = rows[:].bitcast(F32)
        xr16 = xr.bitcast(F16)
        meta32 = meta[:].bitcast(F32)
        pY16, pV16 = pY[:].bitcast(F16), pV[:].bitcast(F16)
        pT16 = pV16[:, 0, 0:4 * P].rearrange("p (k s c) -> p k s c", k=2, s=2)
        pS = pV[:, 1, :].rearrange("p (k s c) -> p k s c", k=2, s=2)

        x_in = [sem(f"x_in{q}") for q in range(NQ)]
        w_in = [sem("w_in0"), sem("w_in1")]
        const_in = sem("const_in")
        pad_out = sem("pad_out")
        w_split_hi = sem("w_split_hi")
        w_split = sem("w_split")
        wp_hi = sem("wp_hi")
        small_split = sem("small_split")
        pool_go = sem("pool_go")
        bo_zero = sem("bo_zero")
        stats_done = sem("stats_done")
        dv = sem("dv")
        var_ready = sem("var_ready")
        root_ready = sem("root_ready")
        xs_ready = sem("xs_ready")
        rows_hi = sem("rows_hi")
        rows_lo = sem("rows_lo")
        turned = sem("turned")
        xt_ready = sem("xt_ready")
        proj_done = sem("proj_done")
        proj_read = sem("proj_read")
        meta_init = sem("meta_init")
        scratch_free = sem("scratch_free")
        gap_ready = sem("gap_ready")
        choice_ready = sem("choice_ready")
        gap_exp = sem("gap_exp")
        cw_ready = sem("cw_ready")
        seg_ready = sem("seg_ready")
        seg_done = sem("seg_done")
        slot_ready = sem("slot_ready")
        tab_ready = sem("tab_ready")
        tab_done = sem("tab_done")
        experts_ready = sem("experts_ready")
        logit_ready = sem("logit_ready")
        logit_exp = sem("logit_exp")
        tsel_ready = sem("tsel_ready")
        table_done = sem("table_done")
        table_ready = sem("table_ready")
        csum_done = sem("csum_done")
        sorted_in = sem("sorted_in")
        l1 = sem("l1")
        silu_done = sem("silu_done")
        hf_done = sem("hf_done")
        hi_done = sem("hi_done")
        lo_done = sem("lo_done")
        lo_early = sem("lo_early")
        l2 = sem("l2")
        y_read = sem("y_read")
        hot_ready = sem("hot_ready")
        aw_ready = sem("aw_ready")
        hot_turned = sem("hot_turned")
        hotT_ready = sem("hotT_ready")
        v_done = sem("v_done")
        v_read = sem("v_read")
        attn_saved = sem("attn_saved")
        attn_added = sem("attn_added")
        d_in = [sem(f"d_in{r}") for r in range(RING)]
        d_turn = sem("d_turn")
        d_meta = sem("d_meta")
        d_xt = sem("d_xt")
        d_l1 = sem("d_l1")
        d_silu = sem("d_silu")
        d_hf = sem("d_hf")
        d_hi = sem("d_hi")
        d_lo = sem("d_lo")
        d_hturn = sem("d_hturn")
        d_hT = sem("d_hT")
        d_l2 = sem("d_l2")
        d_y = sem("d_y")
        d_out = [sem(f"d_out{r}") for r in range(RING)]
        y_in = [sem(f"y_in{r}") for r in range(4)]
        half_sum = sem("half_sum")
        fin = sem("fin")
        out_done = sem("out_done")

        n_const = len(const) + 4
        x_blk = x.rearrange("b (k p j) c -> (b k) p (j c)", p=P, j=TPB)
        out_blk = out.rearrange("b (k p j) c -> (b k) p (j c)", p=P, j=TPB)
        base_blk = base[:].rearrange("p (i j) c -> p i (j c)", j=TPB)
        sorted_steps = sorted_rows.rearrange("(s k p) w -> s p k w", k=2, p=P)
        y_blk = y_rows.rearrange("(k i p j) c -> k i p j c", k=CHOICES, p=P, j=TPB)

        def wait_low(eng, n, early=False):
            if isinstance(n, int) and n < SCATTER_UNIT:
                eng.wait_ge(lo_done, n + 1)
            elif isinstance(n, int) and n >= LAST_LOW:
                eng.wait_ge(lo_early, n + 1 - LAST_LOW + ROUND * ATT - SCATTER_UNIT)
            elif low_by_vector(n) if isinstance(n, int) else early:
                eng.wait_ge(lo_early, n + (1 - SCATTER_UNIT))
            else:
                eng.wait_ge(lo_done, n + (1 - (ROUND * ATT - SCATTER_UNIT)))

        block = ctx.enter_context(nc.Block())

        @block.sync
        def _(sp):
            for q in range(NQ):
                sp.dma_start(base_blk[:, NB // NQ * q:NB // NQ * (q + 1), :],
                             x_blk[NB // NQ * q:NB // NQ * (q + 1)].rearrange("i p w -> p i w")).then_inc(x_in[q], 16)
            sp.wait_ge(const_in, 16 * n_const)
            sp.dma_start(sorted_rows.rearrange("(t p) w -> p t w", p=P),
                         c["pad_row"][:].unsqueeze(1).broadcast_to([P, 2 * STEPS, ROWW])).then_inc(pad_out, 16)

            with sp.Fori(1, NE // 2) as g:
                for r in range(2):
                    sp.wait_ge(w_split, 2 * g + r - 1)
                    sp.dma_start(wraw[:, r, :], wall[bass.ds(2 * g + r, 1)].rearrange("o p w -> p (o w)")
                                 ).then_inc(w_in[r], 16)

            sp.wait_ge(w_split, NE)
            sp.wait_ge(sorted_in, 16 * CHOICES * NT)
            for r in range(RING):
                sp.dma_start(xr[:, r], sorted_steps[r]).then_inc(d_in[r], 16)
            with sp.Fori(1, STEPS // RING) as g:
                for r in range(RING):
                    sp.wait_ge(d_turn, RING * g + (r + 1 - RING))
                    sp.wait_ge(d_meta, RING * g + (r + 1 - RING))
                    sp.dma_start(xr[:, r], sorted_steps[bass.ds(RING * g + r, 1)].rearrange("o p k w -> p (o k) w")
                                 ).then_inc(d_in[r], 16)

            for r in range(RING):
                sp.wait_ge(d_out[r], 2 * 16 * (STEPS // RING))
            for r in range(4):
                for k in range(CHOICES):
                    sp.dma_start(y_all[k][:, TPB * r:TPB * r + TPB, :], y_blk[k, r]).then_inc(y_in[r], 16)
            with sp.Fori(1, NB // 4) as q:
                for r in range(4):
                    sp.wait_ge(y_in[r], 16 * CHOICES * q)
                    for k in range(CHOICES):
                        sp.dma_start(y_all[k][:, bass.ds(16 * q + 4 * r, TPB), :],
                                     y_blk[k, bass.ds(4 * q + r, 1)].rearrange("o p j c -> p (o j) c")
                                     ).then_inc(y_in[r], 16)

        @block.tensor
        def _(pe):
            pe.wait_ge(const_in, 16 * n_const)
            pe.matmul(pY[:, 1, 0:P], c["ones32"][:], wo[:], start=True, stop=True).then_inc(csum_done, 1)

            def turn(g, r):
                i = 4 * g + r
                pe.wait_ge(rows_lo, i + 1)
                if past(i, 2):
                    pe.wait_ge(xt_ready, i - 1)
                for bank, off in ((pA, 0), (pB, P)):
                    for j in range(TPB):
                        mm = pe.matmul(bank[:, r % 2, j * P:(j + 1) * P],
                                       rows16[:, bass.ds(TPB * i + j, 1), off:off + P].rearrange("p o c -> p (o c)"),
                                       c["ident"][:], start=True, stop=True)
                mm.then_inc(turned, 1)

            def project(g, r):
                i = 4 * g + r
                pe.wait_ge(xt_ready, i + 1)
                if past(i, 2):
                    pe.wait_ge(proj_read, i - 1)
                for j in range(TPB):
                    for m, (s, w) in enumerate(((0, 0), (0, 1), (1, 0), (1, 1))):
                        mm = pe.matmul(pV[:, r % 2, j * PROJ:(j + 1) * PROJ],
                                       xT[:, bass.ds(i, 1), s, j * P:(j + 1) * P].rearrange("p o c -> p (o c)"),
                                       wp[:, w, :], start=(m == 0), stop=(m == 3))
                mm.then_inc(proj_done, 1)

            pe.wait_ge(small_split, 1)
            pipeline(pe, NB, 4, 4, [(0, turn), (1, project)])

            def routing_products(g, u):
                n = ROUND * g + u
                if n == SEG_UNIT:
                    pe.wait_ge(seg_ready, 1)
                    pe.matmul(pV[:, 0, 0:E], c["before"][:], seg16[:], start=True, stop=True)
                    pe.matmul(pV[:, 0, 32:32 + E], c["ones"][:], seg16[:], start=True, stop=True).then_inc(seg_done, 1)
                if n == TAB_UNIT:
                    pe.wait_ge(tab_ready, 1)
                    for k in range(2):
                        mm = pe.matmul(pV[0:1, 0, (k + 1) * P:(k + 2) * P], tab16[:, k:k + 1], c["ident"][:],
                                       start=True, stop=True)
                    mm.then_inc(tab_done, 1)
                if n == TABLE_UNIT:
                    pe.wait_ge(tsel_ready, 1)
                    for k in range(2):
                        mm = pe.matmul(pV[:, k, :], c["low_sel"][:],
                                       tsel[:, 8 * k:8 * k + 8, :].rearrange("p b c -> p (b c)"), start=True, stop=True)
                    mm.then_inc(table_done, 1)

            def first_products(b, u):
                n, x, h = 8 * b + u, (u // 2) % 2, u % 2
                if past(n, 2):
                    pe.wait_ge(hf_done, n - 1)
                xi = lambda s: xT[:, bass.ds(2 * b + u // 4, 1), s, :].rearrange("p o c -> p (o c)")
                for bank, col in ((pA, W1), (pB, W3)):
                    w = slice(col + h * P, col + (h + 1) * P)
                    pe.matmul(bank[:, u % 2, :], whi[:, x, w], xi(0), start=True, stop=False)
                    pe.matmul(bank[:, u % 2, :], whi[:, x, w], xi(1), start=False, stop=False)
                    mm = pe.matmul(bank[:, u % 2, :], wlo[:, x, w], xi(0), start=False, stop=True)
                mm.then_inc(l1, 1)

            def second_products(b, u, early=False):
                n, i, x, h = 8 * b + u, 2 * b + u // 4, (u // 2) % 2, u % 2
                w = slice(W2 + h * P, W2 + (h + 1) * P)
                if u % 4 == 0 and past(i, 2):
                    pe.wait_ge(y_read, i - 1)
                wait_low(pe, n, early)
                for j in range(TPB):
                    o, t = pY[:, u // 4, j * P:(j + 1) * P], slice(j * P, (j + 1) * P)
                    if u % 4 == 0:
                        pe.matmul(o, c["ones"][:], bo[:, 0, :], start=(j == 0), stop=False, skip_group_check=True)
                        pe.matmul(o, c["ones"][:], bo[:, 1, :], start=False, stop=False, skip_group_check=True)
                    for m, (hid, wt) in enumerate(((h_hi, whi), (h_hi, wlo), (h_lo, whi))):
                        mm = pe.matmul(o, hid[:, u % 4, t], wt[:, x, w], start=False,
                                       stop=(u % 4 == 3 and m == 2), skip_group_check=True)
                mm.then_inc(l2, 1)

            def turn_hot(g, u):
                m = ROUND * (g - ATT) + u
                if u % 4 == 0:
                    pe.wait_ge(hot_ready, 2 * (g - ATT) + (u // 4 + 1))
                if past(m, 1):
                    pe.wait_ge(hotT_ready, m)
                for k in range(2 * NG):
                    mm = pe.transpose(pV16[:, 0, k * P:(k + 1) * P],
                                      hot[:, u // 4, 2 * (u % 4) + k // NG, k % NG].rearrange("p b h -> p (b h)"),
                                      c["ident"][:])
                mm.then_inc(hot_turned, 1)

            def pick(g, u):
                m = ROUND * (g - ATT) + u
                pe.wait_ge(hotT_ready, m + 1)
                if past(m, 1):
                    pe.wait_ge(v_read, m)
                for k in range(2 * NG):
                    for s in range(2):
                        mm = pe.matmul(pV[:, 1, k * 64:(k + 1) * 64], hotT[:, u % 2, k * P:(k + 1) * P],
                                       table[:, bass.ds(2 * (g - ATT) + u // 4, 1), s, :].rearrange("p o c -> p (o c)"),
                                       start=(s == 0), stop=(s == 1))
                mm.then_inc(v_done, 1)

            pe.wait_ge(w_split, NSH)
            pe.wait_ge(small_split, 2)
            shared = [(0, first_products, 0, UNITS), (3, second_products, 0, UNITS)]
            routing = shared[:1] + [(0, routing_products, 0, UNITS)] + shared[1:]
            both = shared[:1] + [(0, turn_hot, ROUND * ATT, UNITS), (1, pick, ROUND * ATT, UNITS)] + shared[1:]
            straight(0, 2 * ROUND, routing)
            rounds(pe, 2, ATT, shared[:1] + [(3, lambda g, u: second_products(g, u, early=True), 0, UNITS)])
            pe.wait_ge(table_ready, 1)
            straight(ROUND * ATT, ROUND * (ATT + 1), both)
            rounds(pe, ATT + 1, UNITS // ROUND, both)
            straight(UNITS, UNITS + 3, both)

            pe.wait_ge(hotT_ready, APAIRS)

            now = []

            def load_experts(g):
                first = RING * g - 6
                lo = first if past(first, 0) else 0
                n = 8 - (lo - first if isinstance(g, int) else 0)
                _, values = nc.values_load_multi_w_load_instructions(
                    experts[0:1, bass.ds(2 * lo, 2 * n)],
                    engines=(mybir.EngineType.PE,), min_val=NSH, max_val=NE - 1,
                    skip_runtime_bounds_check_because="the table counts 1 to E experts that start at or before a tile")
                now[:] = [None] * (8 - n) + [values[2 * i:2 * i + 2] for i in range(n)]

            def r_turn(g, r):
                pe.wait_ge(d_in[r], 16 * (g + 1))
                if isinstance(g, int) and RING * g + r >= 1:
                    pe.wait_ge(d_xt, RING * g + r)
                for k in range(2):
                    for s in range(2):
                        mm = pe.transpose(pT16[:, k, s, :], xr16[:, r, k, s * P:(s + 1) * P], c["ident"][:])
                mm.then_inc(d_turn, 1)

            def r_first(g, r):
                t = RING * g + r
                if isinstance(g, int):
                    pe.wait_ge(d_xt, t + 1)
                    pe.wait_ge(hf_done, UNITS)
                    if t >= 2:
                        pe.wait_ge(d_hf, t - 1)
                for k, e in enumerate(now[RING + (r + 2) % RING]):
                    o = pAB[:, 2 * (r % 2) + k, :]
                    hi, lo = (wsp[:, s, bass.ds(e, 1), 0:2 * HID].rearrange("p o c -> p (o c)") for s in range(2))
                    pe.matmul(o, xrT[:, r, k, 0, :], hi, start=True, stop=False)
                    pe.matmul(o, xrT[:, r, k, 1, :], hi, start=False, stop=False)
                    mm = pe.matmul(o, xrT[:, r, k, 0, :], lo, start=False, stop=True)
                mm.then_inc(d_l1, 1)

            def r_hturn(g, r):
                t = RING * g + r
                pe.wait_ge(d_lo, t + 1)
                if past(t, 1):
                    pe.wait_ge(d_hT, t)
                else:
                    pe.wait_ge(y_read, NB)
                for s, part in enumerate((h_hi, h_lo)):
                    for k in range(4):
                        mm = pe.transpose(pY16[:, s, k * P:(k + 1) * P],
                                          part[:, r % 2, k * P:(k + 1) * P], c["ident"][:])
                mm.then_inc(d_hturn, 1)

            def r_second(g, r):
                t = RING * g + r
                if isinstance(g, int):
                    pe.wait_ge(d_hT, t + 1)
                if past(t, 1):
                    pe.wait_ge(d_y, t)
                else:
                    pe.wait_ge(v_read, APAIRS)
                for k, e in enumerate(now[(r + 2) % RING]):
                    for h in range(2):
                        w = slice(W2 + h * P, W2 + (h + 1) * P)
                        q = 2 * k + h
                        both = wsp[:, :, bass.ds(e, 1), w].rearrange("p s o c -> p s (o c)")
                        hi = wsp[:, 0, bass.ds(e, 1), w].rearrange("p o c -> p (o c)")
                        pe.matmul(pS[:, k], h_hi[:, 2 + r % 2, q * P:(q + 1) * P], both,
                                  start=(q == 0), stop=False, skip_group_check=True)
                        mm = pe.matmul(pS[:, k, 0, :], h_lo[:, 2 + r % 2, q * P:(q + 1) * P], hi,
                                       start=False, stop=(h == 1), skip_group_check=True)
                mm.then_inc(d_l2, 1)

            pipeline(pe, STEPS, RING, 2, [(6, r_second), (2, r_first), (4, r_hturn), (0, r_turn)], begin=load_experts)

        @block.scalar
        def _(act):
            for dst, src in [(wp_raw[:], wproj), (bp[:], bproj), (wo[:], w_out), (bo_raw[:], b_out)] + [
                    (c[k][:], const[k]) for k in const]:
                act.dma_start(dst, src).then_inc(const_in, 16)
            for r in range(2):
                act.dma_start(wraw[:, r, :], wall[r]).then_inc(w_in[r], 16)
            act.wait_ge(const_in, 16 * n_const)
            nc.scalar.activation(wp[:, 0, :], wp_raw[:], ACT.Copy, scale=WS).then_inc(wp_hi, 1)
            act.wait_ge(bo_zero, 1)

            def split_high(g, r):
                act.wait_ge(w_in[r], 16 * (g + 1))
                nc.scalar.activation(whi[:, bass.ds(2 * g + r, 1), :].rearrange("p o c -> p (o c)"),
                                     wraw[:, r, :], ACT.Copy, scale=WS).then_inc(w_split_hi, 1)

            nc.scalar.activation(bo[0:1, 0, :], bo_raw[:], ACT.Copy, scale=WS).then_inc(wp_hi, 1)
            act.wait_ge(var_ready, 1)
            nc.scalar.activation(st[:, 5, :], st[:, 4, :], ACT.Sqrt).then_inc(root_ready, 1)

            def rows_high(g, r):
                i = 4 * g + r
                act.wait_ge(xs_ready, i + 1)
                nc.scalar.copy(rows16[:, bass.ds(TPB * i, TPB), 0:P], xs[:, r, :, :]).then_inc(rows_hi, 1)

            def turned_copy(g, r):
                i = 4 * g + r
                act.wait_ge(turned, i + 1)
                for s, bank in enumerate((pA, pB)):
                    a = nc.scalar.copy(xT[:, bass.ds(i, 1), s, :].rearrange("p o c -> p (o c)"), bank[:, r % 2, :])
                a.then_inc(xt_ready, 1)

            
            def shared_high(g, r):
                if g == 1 and r < NSH:
                    split_high(0, r)

            pipeline(act, NB, 4, 4, [(0, rows_high), (0, shared_high), (2, turned_copy)])

            def exponentials(g, u):
                n = ROUND * g + u
                if n == GAP_UNIT:
                    act.wait_ge(gap_ready, 1)
                    nc.scalar.activation(rt[:, 5, :], rt[:, 4, :], ACT.Exp).then_inc(gap_exp, 1)
                if n == LOGIT_UNIT:
                    act.wait_ge(logit_ready, 1)
                    nc.scalar.activation(weight, weight, ACT.Exp).then_inc(logit_exp, 1)

            def silu_unit(b, u):
                n = 8 * b + u
                act.wait_ge(l1, n + 1)
                if past(n, 2):
                    act.wait_ge(hf_done, n - 1)
                nc.scalar.activation(silu[:, u % 2, :], pA[:, u % 2, :], ACT.Silu,
                                     scale=1 / (XS * WS)).then_inc(silu_done, 1)

            def hi_unit(b, u):
                n = 8 * b + u
                act.wait_ge(hf_done, n + 1)
                if past(n, 4):
                    act.wait_ge(l2, n - 3)
                nc.scalar.copy(h_hi[:, u % 4, :], hf[:, u % 2, :]).then_inc(hi_done, 1)

            def hot_copy(g, u):
                m = ROUND * (g - ATT) + u
                act.wait_ge(hot_turned, m + 1)
                if past(m, 2):
                    act.wait_ge(v_done, m - 1)
                nc.scalar.copy(hotT[:, u % 2, :], pV16[:, 0, :]).then_inc(hotT_ready, 1)

            def routed_high(g, u):
                if u % 4 == 1:
                    split_high(g - (ATT - 1), u // 4)

            shared = [(0, silu_unit, 0, UNITS), (1, hi_unit, 0, UNITS)]
            routing = shared[:1] + [(0, exponentials, 0, UNITS)] + shared[1:]
            both = shared[:1] + [(0, hot_copy, ROUND * ATT, UNITS)] + shared[1:] + [(0, routed_high, ROUND * ATT, UNITS)]
            straight(0, 2 * ROUND, routing)
            rounds(act, 2, ATT, shared)
            act.wait_ge(scratch_free, 1)
            straight(ROUND * ATT, ROUND * (ATT + 1), both)
            rounds(act, ATT + 1, UNITS // ROUND, both)
            straight(UNITS, UNITS + 3, both)


            def r_xt(g, r):
                t = RING * g + r
                act.wait_ge(d_turn, t + 1)
                nc.scalar.copy(xrT[:, r], pT16).then_inc(d_xt, 1)

            def r_silu(g, r):
                t = RING * g + r
                act.wait_ge(d_l1, t + 1)
                if not past(t, 2):
                    act.wait_ge(hf_done, UNITS)
                    act.wait_ge(l2, UNITS)
                nc.scalar.activation(silu[:, r % 2, :].rearrange("p (k c) -> p k c", k=2),
                                     pAB[:, 2 * (r % 2):2 * (r % 2) + 2, 0:HID], ACT.Silu,
                                     scale=1 / (XS * WS)).then_inc(d_silu, 1)

            def r_hi(g, r):
                t = RING * g + r
                act.wait_ge(d_hf, t + 1)
                nc.scalar.copy(h_hi[:, r % 2, :], hf[:, r % 2, :]).then_inc(d_hi, 1)

            def r_hT(g, r):
                t = RING * g + r
                act.wait_ge(d_hturn, t + 1)
                if isinstance(g, int) and t >= 2:
                    act.wait_ge(d_l2, t - 1)
                nc.scalar.copy(h_hi[:, 2 + r % 2, :], pY16[:, 0, 0:512])
                nc.scalar.copy(h_lo[:, 2 + r % 2, :], pY16[:, 1, 0:512]).then_inc(d_hT, 1)

            pipeline(act, STEPS, RING, 2, [(3, r_silu), (1, r_xt), (5, r_hT), (3, r_hi)])

            with act.Fori(0, NB) as i:
                act.wait_ge(fin, i + 1)
                act.dma_start(out_blk[bass.ds(i, 1)].rearrange("o p w -> p (o w)"),
                              base_blk[:, bass.ds(i, 1), :].rearrange("p o w -> p (o w)")).then_inc(out_done, 16)
            act.wait_ge(out_done, 16 * NB)

        @block.gpsimd
        def _(pool):
            nc.gpsimd.memset(bo[:], 0.0).then_inc(bo_zero, 1)
            nc.gpsimd.memset(rows[:, :, 2 * P // 2:ROWW], 0).then_inc(meta_init, 1)
            pool.wait_ge(const_in, 16 * n_const)
            pool.wait_ge(meta_init, 1)
            nc.gpsimd.tensor_copy(rows[:, :, DEST], c["dest"][:, 0, :]).then_inc(meta_init, 1)

            def rows_low(g, r):
                i = 4 * g + r
                pool.wait_ge(rows_hi, i + 1)
                pool.sem_inc(pool_go, 1)
                nc.gpsimd.tensor_tensor(rows16[:, bass.ds(TPB * i, TPB), P:2 * P], xs[:, r, :, :],
                                        rows16[:, bass.ds(TPB * i, TPB), 0:P], ALU.subtract).then_inc(rows_lo, 1)

            pipeline(pool, NB, 4, 1, [(0, rows_low)])

            early_rows = EARLY_ROWS * (ROUND * ATT - SCATTER_UNIT)

            def rows_due(n):
                if n < ROUND * ATT:
                    return max(0, n + 1 - SCATTER_UNIT) * EARLY_ROWS
                return early_rows + (n + 1 - ROUND * ATT) * (CHOICES * NT - early_rows) // (UNITS - ROUND * ATT)

            for n in range(UNITS):
                if n == SCATTER_UNIT:
                    pool.wait_ge(slot_ready, 1)
                    pool.wait_ge(cw_ready, 1)
                    pool.wait_ge(pad_out, 16)
                for k, t in (divmod(q, NT) for q in range(rows_due(n - 1), rows_due(n))):
                    if k == 1 and t == 0:
                        pool.wait_ge(sorted_in, 16 * NT)
                        nc.gpsimd.tensor_copy(rows[:, :, DEST], c["dest"][:, 1, :]).then_inc(meta_init, 1)
                        nc.gpsimd.tensor_copy(rows32[:, :, CW], cw[:, 1, :]).then_inc(meta_init, 1)
                        pool.wait_ge(meta_init, 4)
                    pool.indirect_dma_start(sorted_rows,
                                            bass.IndirectOffsetOnAxis(ap=slot[:, k, t:t + 1].bitcast(U32), axis=0),
                                            rows[:, t, :], None, bounds_check=SLOTS - 1).then_inc(sorted_in, 16)
                if low_by_vector(n):
                    continue
                pool.wait_ge(hi_done, n + 1)
                nc.gpsimd.tensor_tensor(h_lo[:, n % 4, :], hf[:, n % 2, :], h_hi[:, n % 4, :],
                                        ALU.subtract).then_inc(lo_done, 1)

            def r_scatter(g, r):
                pool.wait_ge(d_y, RING * g + r + 1)
                pool.sem_inc(pool_go, 1)
                for k in range(2):
                    pool.indirect_dma_start(y_rows, bass.IndirectOffsetOnAxis(ap=yidx[:, r, k:k + 1].bitcast(U32), axis=0),
                                            yt[:, r, k, :], None, bounds_check=CHOICES * TOK - 1, oob_is_err=False
                                            ).then_inc(d_out[r], 16)

            pipeline(pool, STEPS, RING, 2, [(6, r_scatter)])

        @block.vector
        def _(dve):
            v = nc.vector
            steps = [0]

            def then(ins):
                steps[0] += 1
                ins.then_inc(dv, 1)
                dve.wait_ge(dv, steps[0])

            def split_low(g, r):
                row = lambda a: a[:, bass.ds(2 * g + r, 1), :].rearrange("p o c -> p (o c)")
                dve.wait_ge(w_split_hi, 2 * g + r + 1)
                v.scalar_tensor_tensor(row(wlo), wraw[:, r, :], WS, row(whi), ALU.mult, ALU.subtract).then_inc(w_split, 1)

            for q in range(NQ):
                dve.wait_ge(x_in[q], 16)
                for t in range(NT // NQ * q, NT // NQ * (q + 1)):
                    ins = v.bn_stats(stats[:, t, :], base[:, t, :])
                ins.then_inc(stats_done, 1)
            dve.wait_ge(stats_done, NQ)
            half = lambda k: stats[:, :, k]
            v.tensor_tensor(st[:, 0, :], half(1), half(4), ALU.add)
            v.tensor_tensor(st[:, 2, :], half(2), half(5), ALU.add)
            then(v.tensor_tensor(st[:, 1, :], half(1), half(4), ALU.subtract))
            then(v.scalar_tensor_tensor(st[:, 3, :], st[:, 1, :], P / 4.0, st[:, 1, :], ALU.mult, ALU.mult))
            then(v.tensor_tensor(st[:, 2, :], st[:, 2, :], st[:, 3, :], ALU.add))
            v.tensor_scalar(st[:, 4, :], st[:, 2, :], 1.0 / P, EPS, ALU.mult, ALU.add).then_inc(var_ready, 1)
            then(v.tensor_scalar(st[:, 0, :], st[:, 0, :], 0.5, None, ALU.mult))
            dve.wait_ge(csum_done, 1)
            then(v.tensor_scalar(csum[:], pY[:, 1, 0:P], 1 / XS, None, ALU.mult))
            dve.wait_ge(wp_hi, 1)
            v.scalar_tensor_tensor(wp[:, 1, :], wp_raw[:], WS, wp[:, 0, :], ALU.mult, ALU.subtract).then_inc(small_split, 1)
            dve.wait_ge(wp_hi, 2)
            v.scalar_tensor_tensor(bo[0:1, 1, :], bo_raw[:], WS, bo[0:1, 0, :], ALU.mult, ALU.subtract).then_inc(small_split, 1)

            dve.wait_ge(root_ready, 1)
            then(v.reciprocal(st[:, 6, :], st[:, 5, :]))
            then(v.tensor_tensor(st[:, 6, :], st[:, 6, :], st[:, 4, :], ALU.mult))
            then(v.tensor_tensor(st[:, 6, :], st[:, 6, :], st[:, 5, :], ALU.add))
            then(v.reciprocal(st[:, 7, :], st[:, 6, :]))
            then(v.tensor_scalar(st[:, 7, :], st[:, 7, :], 2 * XS, None, ALU.mult))

            def normalise(g, r):
                i = 4 * g + r
                if past(i, 4):
                    dve.wait_ge(rows_lo, i - 3)
                for j in range(TPB):
                    t = TPB * i + j
                    ins = v.tensor_scalar(xs[:, r, j, :], base[:, bass.ds(t, 1), :].rearrange("p o c -> p (o c)"),
                                          st[:, 0, bass.ds(t, 1)], st[:, 7, bass.ds(t, 1)], ALU.subtract, ALU.mult)
                ins.then_inc(xs_ready, 1)

            def read_projections(g, r):
                i = 4 * g + r
                dve.wait_ge(proj_done, i + 1)
                v.scalar_tensor_tensor(proj[:, bass.ds(TPB * i, TPB), :],
                                       pV[:, r % 2, 0:TPB * PROJ].rearrange("p (j c) -> p j c", c=PROJ), 1 / (XS * WS),
                                       bp[:].unsqueeze(1).broadcast_to([P, TPB, PROJ]),
                                       ALU.mult, ALU.add).then_inc(proj_read, 1)

            def shared_low(g, r):
                if g == 1 and r >= 4 - NSH:
                    split_low(0, r - (4 - NSH))

            pipeline(dve, NB, 4, 4, [(0, normalise), (0, shared_low), (3, read_projections)])

            def hf_unit(b, u):
                n = 8 * b + u
                dve.wait_ge(silu_done, n + 1)
                if past(n, 2):
                    wait_low(dve, n - 2)
                v.scalar_tensor_tensor(hf[:, u % 2, :], pB[:, u % 2, :], 1 / (XS * WS), silu[:, u % 2, :],
                                       ALU.mult, ALU.mult).then_inc(hf_done, 1)

            def add_shared(b, u):
                if u % 4 != 3:
                    return
                i = 2 * b + u // 4
                dve.wait_ge(l2, 4 * i + 4)
                row = base_blk[:, bass.ds(i, 1), :].rearrange("p o w -> p (o w)")
                v.scalar_tensor_tensor(row, pY[:, u // 4, :], 1 / WS, row, ALU.mult, ALU.add).then_inc(y_read, 1)

            def early_low(b, u):
                n = 8 * b + u
                dve.wait_ge(hi_done, n + 1)
                v.tensor_tensor(h_lo[:, u % 4, :], hf[:, u % 2, :], h_hi[:, u % 4, :],
                                ALU.subtract).then_inc(lo_early, 1)

            shared_parts = [(0, hf_unit, 0, UNITS), (1, early_low, SCATTER_UNIT, ROUND * ATT), (4, add_shared, 0, UNITS)]
            unit = [0]

            def shared_unit():
                straight(unit[0], unit[0] + 1, shared_parts)
                unit[0] += 1

            dve.wait_ge(proj_read, NB)

            logits = proj[:, :, 2 * HP:PROJ]
            wide8 = lambda a: a.unsqueeze(2).broadcast_to([P, NT, E])
            from_last = c["from_last"][:].unsqueeze(1).broadcast_to([P, NT, E])

            def largest(values, eq, score, out_max, out_rank):
                then(v.tensor_reduce(out_max, values, AX.X, ALU.max))
                then(v.tensor_tensor(eq, values, wide8(out_max), ALU.is_equal))
                then(v.tensor_tensor(score, eq, from_last, ALU.mult))
                then(v.tensor_reduce(out_rank, score, AX.X, ALU.max))

            largest(logits, r8[:, 0], r8[:, 1], rt[:, 0, :], rt[:, 1, :])
            shared_unit()
            then(v.tensor_tensor(r8[:, 2], r8[:, 1], wide8(rt[:, 1, :]), ALU.is_equal))
            then(v.scalar_tensor_tensor(r8[:, 3], r8[:, 2], -1e30, logits, ALU.mult, ALU.add))
            shared_unit()
            largest(r8[:, 3], r8[:, 0], r8[:, 1], rt[:, 2, :], rt[:, 3, :])
            v.tensor_tensor(rt[:, 4, :], rt[:, 2, :], rt[:, 0, :], ALU.subtract).then_inc(gap_ready, 1)
            shared_unit()
            v.tensor_tensor(r8[:, 4], r8[:, 1], wide8(rt[:, 3, :]), ALU.is_equal).then_inc(choice_ready, 1)

            by_expert = lambda a: a.rearrange("p t e -> p e t")
            dve.wait_ge(choice_ready, 1)
            then(v.tensor_tensor(member.rearrange("p (e t) -> p e t", e=E), by_expert(r8[:, 2]), by_expert(r8[:, 4]),
                                 ALU.add))
            then(v.tensor_tensor_scan(scan.rearrange("p e t -> p (e t)"), member, member, 0.0, ALU.add, ALU.max))
            then(v.memset(seg[:, 0, :], 0.0))
            then(v.tensor_copy(seg[:, 0, 1:E], scan[:, 0:E - 1, NT - 1]))
            v.tensor_tensor(seg16[:], scan[:, :, NT - 1], seg[:, 0, :], ALU.subtract).then_inc(seg_ready, 1)
            shared_unit()
            dve.wait_ge(gap_exp, 1)
            then(v.tensor_scalar(rt[:, 6, :], rt[:, 5, :], 1.0, None, ALU.add))
            then(v.reciprocal(rt[:, 7, :], rt[:, 6, :]))
            then(v.tensor_scalar(cw[:, 0, :], rt[:, 7, :], 1 / (XS * WS), None, ALU.mult))
            dve.wait_ge(meta_init, 2)
            then(v.tensor_copy(rows32[:, :, CW], cw[:, 0, :]))
            v.tensor_tensor(cw[:, 1, :], cw[:, 0, :], rt[:, 5, :], ALU.mult).then_inc(cw_ready, 1)
            shared_unit()
            assert unit[0] >= SEG_UNIT
            dve.wait_ge(seg_done, 1)
            then(v.tensor_scalar(segi[:, 0, :], pV[:, 0, 32:32 + E], P - 1.0, None, ALU.add))
            then(v.tensor_scalar(segi[:, 1, :], segi[:, 0, :], 7, None, ALU.logical_shift_right))
            then(v.tensor_copy(seg[:, 1, :], segi[:, 1, :]))
            then(v.tensor_tensor_scan(seg[:, 2, :], seg[:, 1, :], seg[:, 1, :], 0.0, ALU.add, ALU.max))
            then(v.tensor_tensor(seg[:, 3, :], seg[:, 2, :], seg[:, 1, :], ALU.subtract))
            then(v.scalar_tensor_tensor(seg[:, 4, :], seg[:, 3, :], float(P), pV[:, 0, 0:E], ALU.mult, ALU.add))
            then(v.scalar_tensor_tensor(seg[:, 5, :], seg[:, 4, :], -1.0, seg[:, 0, :], ALU.add, ALU.subtract))
            then(v.tensor_tensor(place, scan, seg[:, 5, :].unsqueeze(2).broadcast_to([P, E, NT]), ALU.add))
            shared_unit()
            for k, choice in enumerate((r8[:, 2], r8[:, 4])):
                then(v.tensor_tensor(r8[:, 5], choice, place.rearrange("p e t -> p t e"), ALU.mult))
                then(v.tensor_reduce(rt[:, 10 + k, :], r8[:, 5], AX.X, ALU.add))
            v.tensor_copy(slot[:], rt[:, 10:12, :]).then_inc(slot_ready, 1)
            shared_unit()

            for k in range(2):
                then(v.tensor_scalar(tab_scr[:, k, :], seg[:, 3, :], c["tile"][:, k:k + 1], None, ALU.is_le))
            then(v.tensor_reduce(tab_f[:], tab_scr[:], AX.X, ALU.add))
            v.tensor_copy(tab16[:], tab_f[:]).then_inc(tab_ready, 1)
            first_row = xT[:, 0:NB:2, :, 0].unsqueeze(3).broadcast_to([P, BATCH, 2, HI16 * GRP])
            mask = c["high_mask"][:].unsqueeze(1).unsqueeze(1).broadcast_to([P, BATCH, 2, HI16 * GRP])
            dve.wait_ge(xt_ready, NB)
            then(v.tensor_tensor(tsel.rearrange("p (b s) c -> p b s c", s=2), mask, first_row, ALU.mult))
            shared_unit()

            weight4 = weight.rearrange("p t (h k) -> p t h k", k=POINTS)
            wide4 = lambda a: a.unsqueeze(3).broadcast_to([P, NT, HEADS, POINTS])
            then(v.tensor_reduce(wmax[:, 0], weight4, AX.X, ALU.max))
            shared_unit()
            assert unit[0] >= TAB_UNIT
            dve.wait_ge(tab_done, 1)
            then(v.tensor_scalar(experts[:], pV[0:1, 0, P:3 * P], float(NSH - 1), None, ALU.add))
            v.memset(seg[:, 0, 1:2], 0.0).then_inc(tsel_ready, 1)
            v.tensor_tensor(weight4, weight4, wide4(wmax[:, 0]), ALU.subtract).then_inc(logit_ready, 1)
            shared_unit()

            size = scratch_b.rearrange("p (t k) -> p t k", k=HP)
            whole = scratch_a.bitcast(I32).rearrange("p (t k) -> p t k", k=HP)
            fl = [a.rearrange("p (t k) -> p t k", k=HP) for a in fl16]
            idx3 = idx.rearrange("p (t k) -> p t k", k=HP)
            then(v.tensor_scalar(offsets, offsets, 127.5, -128.0, ALU.min, ALU.max))
            shared_unit()
            assert unit[0] >= TABLE_UNIT
            dve.wait_ge(table_done, 1)
            same = c["same_gather"][:].unsqueeze(1).broadcast_to([P, 8, HI16 * GRP])
            for k in range(2):
                ins = v.tensor_tensor(table[:, 4 * k:4 * k + 4].rearrange("p b s c -> p (b s) c"),
                                      pV[:, k, :].rearrange("p (g c) -> p g c", g=8), same, ALU.mult)
            ins.then_inc(table_ready, 1)
            shared_unit()
            then(v.scalar_tensor_tensor(size, offsets, -1.0, offsets, ALU.mult, ALU.max))
            shared_unit()
            then(v.tensor_copy(whole, size))
            shared_unit()
            then(v.scalar_tensor_tensor(fl[0], whole, 0.0, size, ALU.add, ALU.is_gt))
            shared_unit()
            then(v.tensor_tensor(fl[1], whole, fl[0], ALU.subtract))
            shared_unit()
            then(v.tensor_scalar(fl[0], fl[1], -2.0, float(P), ALU.mult, ALU.add))
            then(v.scalar_tensor_tensor(fl[0], offsets, 0.0, fl[0], ALU.is_lt, ALU.mult))
            shared_unit()
            then(v.tensor_tensor(idx3, fl[1], fl[0], ALU.add))
            shared_unit()
            then(v.tensor_scalar(ilo, idx3, LO16 - 1, None, ALU.bitwise_and))
            then(v.tensor_scalar(ihi, idx3, 4, HI16 - 1, ALU.logical_shift_right, ALU.bitwise_and))
            shared_unit()

            assert unit[0] >= LOGIT_UNIT
            dve.wait_ge(logit_exp, 1)
            then(v.tensor_reduce(wmax[:, 1], weight4, AX.X, ALU.add))
            shared_unit()
            then(v.reciprocal(wmax[:, 0], wmax[:, 1]))
            shared_unit()
            then(v.tensor_tensor(weight4, weight4, wide4(wmax[:, 0]), ALU.mult))
            v.memset(seg[:, 0, 0:1], 0.0).then_inc(scratch_free, 1)
            shared_unit()

            def one_hot(g, u):
                batch = 2 * (g - ATT) + (u // 4 + 1)
                if u % 4 == 0 and past(batch, 2):
                    dve.wait_ge(hot_turned, 4 * batch - 4)
                src = proj_i16[:, bass.ds(TPS * batch, TPS), 0:HP].rearrange("p t (g h) -> p t g h", h=GRP)
                for k in range(LO16 // 4 * (u % 4), LO16 // 4 * (u % 4 + 1)):
                    ins = v.tensor_scalar(hot[:, (u // 4 + 1) % 2, :, :, k, :], src, float(k), None, ALU.is_equal)
                if u % 4 == 3:
                    ins.then_inc(hot_ready, 1)

            def weighted_high(g, u):
                half = (ROUND // 2) * (g - ATT) + (u // 2 + 1)
                if u % 2 == 0 and past(half, 2):
                    dve.wait_ge(v_read, 2 * half - 2)
                tiles = bass.ds(TPB * half, TPB)
                src = proj_i16[:, tiles, HP:2 * HP].rearrange("p t (g h) -> p t g h", h=GRP)
                w = proj[:, tiles, HP:2 * HP].rearrange("p t (g h) -> p t g h", h=GRP)
                for k in range(HI16 // 2 * (u % 2), HI16 // 2 * (u % 2 + 1)):
                    ins = v.scalar_tensor_tensor(aw[:, (u // 2 + 1) % 2, :, :, k, :], src, float(k), w,
                                                 ALU.is_equal, ALU.mult)
                if u % 2 == 1:
                    ins.then_inc(aw_ready, 1)

            def weigh(g, u):
                m = ROUND * (g - ATT) + u
                if u % 4 == 0 and past(m, 8):
                    dve.wait_ge(attn_saved, 2 * (g - ATT) + (u // 4 - 1))
                if u % 2 == 0:
                    dve.wait_ge(aw_ready, (ROUND // 2) * (g - ATT) + (u // 2 + 1))
                dve.wait_ge(v_done, m + 1)
                for t in range(2):
                    ins = v.tensor_tensor_reduce(vscr[:, t, :], pV[:, 1, t * 256:(t + 1) * 256],
                                                 aw[:, (u // 2) % 2, 2 * (u % 2) + t].rearrange("p g a h -> p (g a h)"),
                                                 1.0, 0.0, ALU.mult, ALU.add,
                                                 attn[:, u // 4, 2 * (u % 4) + t:2 * (u % 4) + t + 1])
                ins.then_inc(v_read, 1)

            def keep_sums(g, u):
                if u % 4 == 3:
                    m = ROUND * (g - ATT) + u
                    dve.wait_ge(v_read, m + 1)
                    v.tensor_copy(attn_all[:, bass.ds(ROUND * (2 * (g - ATT) + u // 4), 8)],
                                  attn[:, u // 4, :]).then_inc(attn_saved, 1)

            def routed_low(g, u):
                if u % 4 == 2:
                    split_low(g - (ATT - 1), u // 4)

            while unit[0] < ROUND * ATT - 4:
                shared_unit()
            for u in range(ROUND - 4, ROUND):
                shared_unit()
                one_hot(ATT - 1, u)
                if u >= ROUND - 2:
                    weighted_high(ATT - 1, u)

            start, end = ROUND * ATT, UNITS
            both = shared_parts[:2] + [(1, early_low, LAST_LOW, UNITS), (0, one_hot, start, end - 4), (1, weigh, start, end),
                                       (0, weighted_high, start, end - 2), (1, keep_sums, start, end),
                                       (0, routed_low, start, end)] + shared_parts[2:]
            straight(start, start + ROUND, both)
            rounds(dve, ATT + 1, UNITS // ROUND - 1, both[:1] + both[3:])
            straight(UNITS - ROUND, UNITS + 4, both)

            wait_low(dve, UNITS - 1)

            def r_meta(g, r):
                dve.wait_ge(d_in[r], 16 * (g + 1))
                if past(RING * g + r, RING):
                    dve.wait_ge(d_y, RING * g + r - RING + 1)
                v.tensor_copy(meta[:, r], xr[:, r, :, CW:CW + 2]).then_inc(d_meta, 1)

            def r_hf(g, r):
                t = RING * g + r
                dve.wait_ge(d_meta, t + 1)
                dve.wait_ge(d_silu, t + 1)
                for k in range(2):
                    ins = v.scalar_tensor_tensor(hf[:, r % 2, k * HID:(k + 1) * HID],
                                                 pAB[:, 2 * (r % 2) + k, HID:2 * HID], meta32[:, r, k, 0:1],
                                                 silu[:, r % 2, k * HID:(k + 1) * HID], ALU.mult, ALU.mult)
                ins.then_inc(d_hf, 1)

            def r_lo(g, r):
                t = RING * g + r
                dve.wait_ge(d_hi, t + 1)
                v.tensor_tensor(h_lo[:, r % 2, :], hf[:, r % 2, :], h_hi[:, r % 2, :], ALU.subtract).then_inc(d_lo, 1)

            def r_y(g, r):
                t = RING * g + r
                dve.wait_ge(d_l2, t + 1)
                if past(t, RING):
                    dve.wait_ge(d_out[r], 2 * 16 * g)
                v.tensor_reduce(yt[:, r], pS.rearrange("p k s c -> p k c s"), AX.X, ALU.add)
                v.tensor_copy(yidx[:, r, :], meta[:, r, :, 1]).then_inc(d_y, 1)

            def add_attention(tile):
                row = base[:, bass.ds(tile, 1), :].rearrange("p o c -> p (o c)")
                return v.scalar_tensor_tensor(row, csum[:], attn_all[:, bass.ds(tile, 1)], row, ALU.mult, ALU.add)

            peel = 2
            for_each = STEPS // RING - peel
            adds = NT // for_each

            def r_attention(g, r):
                if not isinstance(g, int):
                    for tile in range(adds * r // RING, adds * (r + 1) // RING):
                        add_attention(adds * (g - peel) + tile)

            dve.wait_ge(y_read, NB)
            dve.wait_ge(attn_saved, BATCH)
            pipeline(dve, STEPS, RING, peel, [(4, r_lo), (3, r_hf), (6, r_y), (2, r_meta), (0, r_attention)])
            for tile in range(adds * for_each, NT):
                ins = add_attention(tile)
            ins.then_inc(attn_added, 1)

            dve.wait_ge(attn_added, 1)
            dve.wait_ge(y_read, NB)
            with dve.Fori(0, NB // 4) as q:
                for r in range(4):
                    dve.wait_ge(y_in[r], 16 * CHOICES * (q + 1))
                    tiles = base[:, bass.ds(4 * (4 * q + r), TPB), :]
                    for k in range(CHOICES):
                        if k:
                            dve.wait_ge(half_sum, 4 * q + (r + 1))
                        ins = v.scalar_tensor_tensor(tiles, y_all[k][:, bass.ds(4 * (4 * q + r), TPB), :], 1 / WS, tiles,
                                                     ALU.mult, ALU.add).then_inc(fin if k else half_sum, 1)


def kernel(**inputs):
    import concourse.bacc as _bacc
    from concourse.bass_utils import run_bass_kernel_spmd as _run

    a = {k.replace("L0_attn_", "").replace("L0_ffn_", "f_"): np.asarray(v) for k, v in inputs.items()}
    wproj = np.concatenate([a["W_off"][:, 0::2], a["W_attn"], a["f_router_w"].T], axis=1)
    bproj = np.concatenate([a["b_off"][0::2], a["b_attn"], a["f_expert_bias"]])
    w1 = np.concatenate([a["f_sw1"], a["f_w1"]])
    w3 = np.concatenate([a["f_sw3"], a["f_w3"]])
    w2 = np.concatenate([a["f_sw2"], a["f_w2"]])
    by_half = w2.transpose(0, 2, 1).reshape(NE, HID // P, P, P).transpose(0, 2, 1, 3).reshape(NE, P, HID)
    wall = np.concatenate([w1.transpose(0, 2, 1), w3.transpose(0, 2, 1), by_half], axis=2)
    const = constants()
    arrays = {
        "x": a["x"], "wall": wall, "wproj": wproj, "bproj": np.broadcast_to(bproj[None, :], (P, PROJ)),
        "w_out": a["W_out"], "b_out": a["b_out"][None, :],
    }
    arrays = {k: np.ascontiguousarray(v) for k, v in arrays.items()}
    arrays |= {"c_" + k: np.ascontiguousarray(v) for k, v in const.items()}

    nc = _bacc.Bacc("TRN2", target_bir_lowering=False, num_devices=1)
    dram = {k: nc.dram_tensor("in_" + k, v.shape, mybir.dt.from_np(v.dtype), kind="ExternalInput").ap()
            for k, v in arrays.items()}
    out = nc.dram_tensor("out_dram", a["x"].shape, F32, kind="ExternalOutput").ap()
    sorted_rows = nc.dram_tensor("sorted_rows", [SLOTS, ROWW], I32, kind="Internal").ap()
    y_rows = nc.dram_tensor("y_rows", [CHOICES * TOK, P], F32, kind="Internal").ap()
    consts = {k: dram["c_" + k] for k in const}
    layer_kernel(nc, dram["x"], dram["wall"], dram["wproj"], dram["bproj"], dram["w_out"], dram["b_out"],
                 consts, out, sorted_rows, y_rows)
    got = _run(nc, [{"in_" + k: v for k, v in arrays.items()}], core_ids=[0])
    return got.results[0]["out_dram"]
```
